# Optimizing a Trainium2 kernel written in Bass

```python
import numpy as np
import jax
import jax.numpy as jnp

def _softmax(x, axis=-1):
    return jax.nn.softmax(x, axis=axis)

def _gelu(x):
    return jax.nn.gelu(x, approximate=True)

def _silu(x):
    return jax.nn.silu(x)

def _sigmoid(x):
    return jax.nn.sigmoid(x)

def _layernorm(x, axis=-1, eps=1e-05):
    m = jnp.mean(x, axis=axis, keepdims=True)
    v = jnp.var(x, axis=axis, keepdims=True)
    return (x - m) / jnp.sqrt(v + eps)

def _scatter_add(tgt, idx, src, axis=0):
    return tgt.at[idx].add(src)

def _segment_sum(src, seg, n):
    return jax.ops.segment_sum(src, seg, n)
kernel_name = 'mk_adj_ffn_d2_adj_r2_13e86f'

def setup_inputs(seed: int=0):
    np.random.seed(seed)
    _w = jnp.asarray

    def _rec_inputs():
        import jax
        import jax.numpy as jnp
        _gk = jax.random.key(seed)
        x = -0.0002928 + 1 * jax.random.normal(jax.random.fold_in(_gk, 1), (128, 128, 128), jnp.float32)
        _w = (1.0 + jnp.arange(128, dtype=jnp.float32)) ** (-0.5)
        _w = _w / _w.mean()
        _pij = jnp.clip(0.03125 * _w[:, None] * _w[None, :], 0.0, 1.0)
        _a = jax.random.uniform(jax.random.fold_in(_gk, 2), (128, 128)) < _pij
        adj = _a.astype(jnp.int32)
        return (x, adj)
    x, adj = _rec_inputs()

    def _L0_gnn_setup():
        import jax, jax.numpy as jnp
        import numpy as np
        NEG_BIG = -9000000000000000.0
        key = jax.random.key(seed)
        k1, k2, k3, k4 = jax.random.split(key, 4)
        bs, N, Fin, Fout = (8, 1024, 128, 128)
        x = jax.random.normal(k1, (bs, N, Fin), dtype=jnp.float32)
        adj = jax.random.randint(k2, (N, N), 0, 2, dtype=jnp.int32)
        W = jax.random.normal(k3, (Fin, Fout), dtype=jnp.float32) * (1.414 / np.sqrt(Fin))
        a = jax.random.normal(k4, (2 * Fout, 1), dtype=jnp.float32) * 0.1
        return {'x': x, 'adj': adj, 'W': W, 'a': a}
    _L0_gnn_all = _L0_gnn_setup()
    _L0_gnn_in = {k: v for k, v in _L0_gnn_all.items() if k in ('W', 'a')}
    del _L0_gnn_all

    def _L0_ffn_setup():
        import jax, jax.numpy as jnp
        import numpy as np
        E = 8
        K = 2
        D = 128
        H = 256
        DOUT = 128
        EPS = 1e-05
        key = jax.random.key(seed)
        ks = jax.random.split(key, 9)
        s = 0.02
        return {'x': jax.random.normal(ks[0], (4, 4096, D), jnp.float32), 'gamma': 1.0 + 0.05 * jax.random.normal(ks[1], (D,), jnp.float32), 'beta': 0.05 * jax.random.normal(ks[2], (D,), jnp.float32), 'Wr': 0.01 * jax.random.normal(ks[3], (D, E), jnp.float32), 'br': jnp.zeros((E,), jnp.float32), 'W1': s * jax.random.normal(ks[4], (E, D, H), jnp.float32), 'b1': s * jax.random.normal(ks[5], (E, H), jnp.float32), 'W2': s * jax.random.normal(ks[6], (E, H, DOUT), jnp.float32), 'b2': s * jax.random.normal(ks[7], (E, DOUT), jnp.float32)}
    _L0_ffn_all = _L0_ffn_setup()
    _L0_ffn_in = {k: v for k, v in _L0_ffn_all.items() if k in ('gamma', 'beta', 'Wr', 'br', 'W1', 'b1', 'W2', 'b2')}
    del _L0_ffn_all

    def _L1_gnn_setup():
        import jax, jax.numpy as jnp
        import numpy as np
        IN_F = 128
        OUT_F = 128
        ALPHA = 0.01
        NEG_INF = -1000000000.0
        key = jax.random.key(seed)
        k_inp, k_adj, k_W, k_a = jax.random.split(key, 4)
        inp = jax.random.normal(k_inp, (8, 1024, IN_F), dtype=jnp.float32)
        adj = jax.random.randint(k_adj, (1024, 1024), 0, 2, dtype=jnp.int32)
        gain = 1.414
        lim_W = gain * np.sqrt(6.0 / (IN_F + OUT_F))
        W = jax.random.uniform(k_W, (IN_F, OUT_F), minval=-lim_W, maxval=lim_W, dtype=jnp.float32)
        lim_a = gain * np.sqrt(6.0 / (2 * OUT_F + 1))
        a = jax.random.uniform(k_a, (2 * OUT_F, 1), minval=-lim_a, maxval=lim_a, dtype=jnp.float32)
        return {'inp': inp, 'adj': adj, 'W': W, 'a': a}
    _L1_gnn_all = _L1_gnn_setup()
    _L1_gnn_in = {k: v for k, v in _L1_gnn_all.items() if k in ('W', 'a')}
    del _L1_gnn_all

    def _L1_ffn_setup():
        import jax, jax.numpy as jnp
        import numpy as np
        B, K, D = (256, 16, 128)
        E = 32
        H = int(D * 0.25)
        key = jax.random.key(seed)
        ks = jax.random.split(key, 7)
        d_rs = D ** (-0.5)
        h_rs = H ** (-0.5)
        x = jax.random.normal(ks[0], (B, K, D), dtype=jnp.float32)
        router_w = jax.random.uniform(ks[1], (E, D), jnp.float32, -d_rs, d_rs)
        router_b = jax.random.uniform(ks[2], (E,), jnp.float32, -d_rs, d_rs)
        W1 = jax.random.uniform(ks[3], (E, D, H), jnp.float32, -h_rs, h_rs)
        b1 = jax.random.uniform(ks[4], (E, H), jnp.float32, -h_rs, h_rs)
        W2 = jax.random.uniform(ks[5], (E, H, D), jnp.float32, -d_rs, d_rs)
        b2 = jax.random.uniform(ks[6], (E, D), jnp.float32, -d_rs, d_rs)
        return {'x': x, 'router_w': router_w, 'router_b': router_b, 'W1': W1, 'b1': b1, 'W2': W2, 'b2': b2}
    _L1_ffn_all = _L1_ffn_setup()
    _L1_ffn_in = {k: v for k, v in _L1_ffn_all.items() if k in ('router_w', 'router_b', 'W1', 'b1', 'W2', 'b2')}
    del _L1_ffn_all
    return {'x': x, 'adj': adj, 'L0_gnn_W': _L0_gnn_in['W'], 'L0_gnn_a': _L0_gnn_in['a'], 'L0_ffn_gamma': _L0_ffn_in['gamma'], 'L0_ffn_beta': _L0_ffn_in['beta'], 'L0_ffn_Wr': _L0_ffn_in['Wr'], 'L0_ffn_br': _L0_ffn_in['br'], 'L0_ffn_W1': _L0_ffn_in['W1'], 'L0_ffn_b1': _L0_ffn_in['b1'], 'L0_ffn_W2': _L0_ffn_in['W2'], 'L0_ffn_b2': _L0_ffn_in['b2'], 'L1_gnn_W': _L1_gnn_in['W'], 'L1_gnn_a': _L1_gnn_in['a'], 'L1_ffn_router_w': _L1_ffn_in['router_w'], 'L1_ffn_router_b': _L1_ffn_in['router_b'], 'L1_ffn_W1': _L1_ffn_in['W1'], 'L1_ffn_b1': _L1_ffn_in['b1'], 'L1_ffn_W2': _L1_ffn_in['W2'], 'L1_ffn_b2': _L1_ffn_in['b2']}

def reference(x, adj, L0_gnn_W, L0_gnn_a, L0_ffn_gamma, L0_ffn_beta, L0_ffn_Wr, L0_ffn_br, L0_ffn_W1, L0_ffn_b1, L0_ffn_W2, L0_ffn_b2, L1_gnn_W, L1_gnn_a, L1_ffn_router_w, L1_ffn_router_b, L1_ffn_W1, L1_ffn_b1, L1_ffn_W2, L1_ffn_b2):
    import jax
    import jax.numpy as jnp

    def _L0_gnn_ref(x, adj, W, a):
        import jax, jax.numpy as jnp
        import numpy as np
        NEG_BIG = -9000000000000000.0
        alpha = 0.2
        h = jnp.matmul(x, W)
        Fout = h.shape[-1]
        a1, a2 = (a[:Fout, 0], a[Fout:, 0])
        s1 = jnp.einsum('bnf,f->bn', h, a1)
        s2 = jnp.einsum('bnf,f->bn', h, a2)
        e = jax.nn.leaky_relu(s1[:, :, None] + s2[:, None, :], negative_slope=alpha)
        attention = jnp.where(adj[None, :, :] > 0, e, NEG_BIG)
        attention = jax.nn.softmax(attention, axis=-1)
        h_prime = jnp.matmul(attention, h)
        return jax.nn.elu(h_prime)

    def _L0_ffn_ref(x, gamma, beta, Wr, br, W1, b1, W2, b2):
        import jax, jax.numpy as jnp
        import numpy as np
        E = 8
        K = 2
        D = 128
        H = 256
        DOUT = 128
        EPS = 1e-05
        mu = jnp.mean(x, axis=-1, keepdims=True)
        var = jnp.mean(jnp.square(x - mu), axis=-1, keepdims=True)
        xn = (x - mu) * jax.lax.rsqrt(var + EPS) * gamma + beta
        logits = jnp.einsum('bsd,de->bse', xn, Wr) + br
        top_vals, top_idx = jax.lax.top_k(logits, K)
        w = jax.nn.softmax(top_vals, axis=-1)
        w_full = jnp.einsum('bsk,bske->bse', w, jax.nn.one_hot(top_idx, E, dtype=w.dtype))
        y = jnp.zeros(x.shape[:-1] + (DOUT,), x.dtype)
        for e in range(E):
            h = jax.nn.gelu(jnp.einsum('bsd,dh->bsh', xn, W1[e]) + b1[e], approximate=False)
            y_e = jnp.einsum('bsh,hd->bsd', h, W2[e]) + b2[e]
            y = y + y_e * w_full[..., e, None]
        return y

    def _L1_gnn_ref(inp, adj, W, a):
        import jax, jax.numpy as jnp
        import numpy as np
        IN_F = 128
        OUT_F = 128
        ALPHA = 0.01
        NEG_INF = -1000000000.0
        h = jnp.matmul(inp, W)
        a1 = a[:OUT_F, 0]
        a2 = a[OUT_F:, 0]
        e_src = jnp.einsum('bnf,f->bn', h, a1)
        e_dst = jnp.einsum('bnf,f->bn', h, a2)
        e = jax.nn.leaky_relu(e_src[:, :, None] + e_dst[:, None, :], negative_slope=ALPHA)
        e = jnp.where(adj[None, :, :] == 0, NEG_INF, e)
        attention = jax.nn.softmax(e, axis=-1)
        h_prime = jnp.matmul(attention, h)
        return jax.nn.relu(h_prime)

    def _L1_ffn_ref(x, router_w, router_b, W1, b1, W2, b2):
        import jax, jax.numpy as jnp
        import numpy as np
        B, K, D = (256, 16, 128)
        E = 32
        H = int(D * 0.25)
        xf = x.reshape(-1, D)
        logits = xf @ router_w.T + router_b
        idx = jnp.argmax(logits, axis=-1)
        w1t = jnp.take(W1, idx, axis=0)
        h = jnp.einsum('nd,ndh->nh', xf, w1t) + jnp.take(b1, idx, axis=0)
        h = jax.nn.relu(h)
        w2t = jnp.take(W2, idx, axis=0)
        out = jnp.einsum('nh,nhd->nd', h, w2t) + jnp.take(b2, idx, axis=0)
        out = jax.nn.relu(out)
        return out.reshape(x.shape)
    x = x + _L0_gnn_ref(_layernorm(x, axis=-1), adj, L0_gnn_W, L0_gnn_a)
    x = x + _L0_ffn_ref(_layernorm(x, axis=-1), L0_ffn_gamma, L0_ffn_beta, L0_ffn_Wr, L0_ffn_br, L0_ffn_W1, L0_ffn_b1, L0_ffn_W2, L0_ffn_b2)
    x = x + _L1_gnn_ref(_layernorm(x, axis=-1), adj, L1_gnn_W, L1_gnn_a)
    x = x + _L1_ffn_ref(_layernorm(x, axis=-1), L1_ffn_router_w, L1_ffn_router_b, L1_ffn_W1, L1_ffn_b1, L1_ffn_W2, L1_ffn_b2)
    return x

_drawn_inputs = setup_inputs


def setup_inputs(seed=0):
    import zlib

    import numpy as np

    out = dict(_drawn_inputs(seed))
    spreads = {'L0_ffn_br': (0.0, 0.268)}
    factors = {'L0_ffn_gamma': 8.0,
     'L0_ffn_beta': 8.0,
     'L0_ffn_Wr': 3.211,
     'L0_ffn_b1': 8.0,
     'L0_ffn_b2': 3.821,
     'L1_ffn_b1': 7.033,
     'L1_ffn_b2': 2.816}
    for name, (base, spread) in spreads.items():
        noise = np.random.default_rng([zlib.crc32(name.encode()), seed]).standard_normal(out[name].shape)
        drawn = base * np.exp(spread * noise) if base else spread * noise
        out[name] = jnp.asarray(drawn.astype(out[name].dtype))
    for name, factor in factors.items():
        out[name] = (out[name] * factor).astype(out[name].dtype)
    return out
```

```python
from contextlib import ExitStack

import concourse.bass as bass
from concourse import mybir

F32 = mybir.dt.float32
F32R = mybir.dt.float32r
BF16 = mybir.dt.bfloat16
I32 = mybir.dt.int32
U32 = mybir.dt.uint32
ALU = mybir.AluOpType
ACT = mybir.ActivationFunctionType
AX = mybir.AxisListType

P = 128
NGRAPH = 128
G = 4
T = G * P
NGROUP = NGRAPH // G
E0, H0 = 8, 256
C0 = H0 // P
E1, H1 = 32, 32
NCH = E1 * H1 // P
SLOTS = 8
assert E0 == SLOTS and NCH == SLOTS
EPS = 1e-5
SLOPE = (0.2, 0.01)
MASKED = -1e30

LAG = dict(A=0, B=1, C=2, D=3, E=4, F=5, M=6, O=7)
NITER = NGROUP + LAG["O"]
FIRST = 10


class At:

    def __init__(self, j, p, lag):
        self.j, self.p, self.lag = j, p, lag
        self.n = 2 * j + (p - lag)
        self.fixed = isinstance(j, int)

    @property
    def par(self):
        return (self.p - self.lag) % 2

    @property
    def half(self):
        return self.j + (self.p - self.lag) // 2

    def live(self):
        return not self.fixed or 0 <= self.n < NGROUP

    def before(self, k):
        return At(self.j, self.p, self.lag + k)

    def count(self, per, k):
        if not self.fixed:
            return per * self.n + k
        if self.n < 0:
            return None
        return per * NGROUP if self.n >= NGROUP else per * self.n + k


def program(nc, x, adj, W_0, a_0, gamma, beta, Wr, br, W1_0, b1_0, W2_0, b2_0,
            W_1, a_1, rw, rb, W1_1, b1_1, W2_1, b2_1, out):
    ctx = ExitStack()
    with ctx:
        def sb(name, shape, dt=F32):
            return ctx.enter_context(nc.sbuf_tensor(name, shape, dt))

        def pb(name):
            return ctx.enter_context(nc.psum_tensor(name, [P, T], F32))

        sems = {}

        def sem(name):
            if name not in sems:
                sems[name] = ctx.enter_context(nc.semaphore(name))
            return sems[name]

        def after(eng, name, g, per=1, k=1):
            v = g.count(per, k)
            if v is not None:
                eng.wait_ge(sem(name), v)

        def settle():
            nc.vector.memset(spare[:, :], 0.0)

        ident = sb("ident", [P, P])
        identb = sb("identb", [P, P], BF16)
        mask = [sb(f"mask{l}", [P, P], BF16) for l in range(2)]
        adj_i = sb("adj_i", [P, P], I32)
        adj_f = sb("adj_f", [P, P])
        adj_m = sb("adj_m", [P, 2, P])
        Wg = [sb(f"Wg{l}", [P, P]) for l in range(2)]
        arow = sb("arow", [P, 2, 2, P])
        wprod = sb("wprod", [P, 2, 2, P])
        wa = sb("wa", [P, 2, 2])
        ones = sb("ones", [P, P])
        wa2rep = [sb(f"wa2rep{l}", [P, P]) for l in range(2)]
        gcol = sb("gcol", [P, 1])
        bcol = sb("bcol", [P, 1])
        b1col = sb("b1col", [P, E0 * C0])
        b1row = sb("b1row", [E0 * C0, P])
        wr_sb = sb("wr_sb", [P, E0])
        brow = sb("brow", [P, E0])
        rw_row = sb("rw_row", [E1, P])
        rwT = sb("rwT", [P, E1])
        rbrow = sb("rbrow", [P, E1])
        iota_i = sb("iota_i", [P, E1], I32)
        iota = sb("iota", [P, E1])
        spare = sb("spare", [P, 1])
        eps = sb("eps", [P, G])
        neghalf = sb("neghalf", [P, G])
        w1raw = sb("w1raw", [P, E0 * H0])
        w1hi = sb("w1hi", [P, E0 * H0], F32R)
        w1lo = sb("w1lo", [P, E0 * H0], F32R)
        w2 = sb("w2", [P, E0 * C0, P])
        b2raw = sb("b2raw", [64, E0 * P])
        b2hi = sb("b2hi", [64, E0 * P], F32R)
        b2c = sb("b2c", [64, E0 * P], F32R)
        ones_r = sb("ones_r", [64, P], F32R)
        v1raw = sb("v1raw", [P, E1 * H1])
        v1hi = sb("v1hi", [P, E1 * H1], F32R)
        v1lo = sb("v1lo", [P, E1 * H1], F32R)
        v2 = sb("v2", [P, NCH, P])
        c2raw = sb("c2raw", [64, P])
        c2hi = sb("c2hi", [64, P], F32R)
        c2 = sb("c2", [64, P], F32R)
        selraw = sb("selraw", [96, E1 * H1])
        selhi = sb("selhi", [96, E1 * H1], F32R)
        sel = sb("sel", [96, E1 * H1], F32R)

        x0 = [sb(f"x0_{p}", [P, G, P]) for p in range(2)]
        x1 = [sb(f"x1_{p}", [P, G, P]) for p in range(2)]
        x2 = [sb(f"x2_{p}", [P, G, P]) for p in range(2)]
        x3 = [sb(f"x3_{p}", [P, G, P]) for p in range(2)]
        fin = [sb(f"fin{p}", [P, G, P]) for p in range(2)]
        st = {k: sb(f"st{k}", [P, G, 6]) for k in "ACEF"}
        mv = {k: sb(f"mv{k}", [P, G, 2]) for k in "ACEF"}
        ve = {k: sb(f"ve{k}", [P, G]) for k in "ACEF"}
        rs = {k: sb(f"rs{k}", [P, G]) for k in "ACEF"}
        v2t = sb("v2t", [P, 4, G])
        xn = {k: sb(f"xn{k}", [P, G, P]) for k in "ACEF"}
        xnT = {k: sb(f"xnT{k}", [P, T]) for k in "ACEF"}
        hg = {k: [sb(f"hg{k}{p}", [P, G, P]) for p in range(2)] for k in "AE"}
        s1 = {k: sb(f"s1{k}", [P, G]) for k in "AE"}
        tt = {k: sb(f"tt{k}", [P, G, P]) for k in "AE"}
        ee = {k: sb(f"ee{k}", [P, G, P]) for k in "AE"}
        em = {k: sb(f"em{k}", [P, G]) for k in "AE"}
        sc = {k: sb(f"sc{k}", [P, G, P]) for k in "AE"}
        pr = {k: sb(f"pr{k}", [P, G, P]) for k in "BF"}
        prT = {k: sb(f"prT{k}", [P, T]) for k in "BF"}
        rsum = {k: sb(f"rsum{k}", [P, G]) for k in "BF"}
        rinv = {k: sb(f"rinv{k}", [P, G]) for k in "BF"}
        z = {k: sb(f"z{k}", [P, G, P]) for k in "BF"}
        zneg = sb("zneg", [P, G, P])
        eneg = sb("eneg", [P, G, P])
        x1a = sb("x1a", [P, G, P])
        xhi = {k: [sb(f"xhi{k}{p}", [P, T], F32R) for p in range(2)] for k in "CF"}
        xlo = {k: [sb(f"xlo{k}{p}", [P, T], F32R) for p in range(2)] for k in "CF"}
        lg = {"C": sb("lgC", [P, G, E0]), "F": sb("lgF", [P, G, E1])}
        top = {k: sb(f"top{k}", [P, G, 8]) for k in "CF"}
        idx = {k: sb(f"idx{k}", [P, G, 8], U32) for k in "CF"}
        idf = {k: sb(f"idf{k}", [P, G, 2]) for k in "CF"}
        dif = sb("dif", [P, G])
        th = sb("th", [P, G])
        w01 = sb("w01", [P, 2, G])
        oh2 = sb("oh2", [P, 2, G, E0])
        ohw = sb("ohw", [P, 2, G, E0])
        wgt = [sb(f"wgt{p}", [P, G, E0]) for p in range(2)]
        ohc = sb("ohc", [P, G, 3 * E1])
        ohT = [sb(f"ohT{p}", [3 * E1, T], F32R) for p in range(2)]
        hid = [[sb(f"hid{s}{c}", [P, T]) for c in range(C0)] for s in range(2)]
        ym = [sb(f"ym{s}", [P, G, P]) for s in range(2)]
        acc = sb("acc", [P, G, P])
        rel = [sb(f"rel{s}", [P, T]) for s in range(2)]
        oT = sb("oT", [P, T])

        ZB = [pb("Z0"), pb("Z1")]
        YB = pb("Y")
        OB = pb("O")
        TP0 = pb("TP0")
        TP1 = pb("TP1")
        HB = pb("H")
        SB = pb("S")
        TPB = dict(A=TP0, B=TP0, C=TP0, E=TP1, F=TP1)

        def g4(t):
            return t[:, :].rearrange("p (g f) -> p g f", g=G)

        def each(body):
            def run(eng, *a):
                for i in range(FIRST):
                    body(i // 2, i % 2)
                with eng.Fori(FIRST // 2, NGROUP // 2) as j:
                    for p in range(2):
                        body(j, p)
                for i in range(NGROUP, NITER):
                    body(i // 2, i % 2)
            return run

        NCONST = 18
        xg = x.rearrange("(n g) t f -> n t g f", g=G)
        og = out.rearrange("(n g) t f -> n t g f", g=G)
        block = ctx.enter_context(nc.Block())

        @block.sync
        def _(sp):
            def const(dst, src):
                sp.dma_start(dst, src).then_inc(sem("const_in"), 16)

            const(adj_i[:, :], adj)
            const(Wg[0][:, :], W_0)
            const(Wg[1][:, :], W_1)
            for l, a in enumerate((a_0, a_1)):
                const(arow[:, l, :, :], a.rearrange("(o k f) u -> o k (f u)", o=1, k=2).broadcast_to([P, 2, P]))
            const(gcol[:, :], gamma.rearrange("(p u) -> p u", u=1))
            const(bcol[:, :], beta.rearrange("(p u) -> p u", u=1))
            const(b1row[:, :], b1_0.rearrange("e (c p) -> (e c) p", c=C0))
            const(wr_sb[:, :], Wr)
            const(brow[:, :], br.rearrange("(u e) -> u e", u=1).broadcast_to([P, E0]))
            const(rw_row[:, :], rw)
            const(rbrow[:, :], rb.rearrange("(u e) -> u e", u=1).broadcast_to([P, E1]))
            const(w1raw[:, :].rearrange("p (e h) -> p e h", e=E0), W1_0.rearrange("e d h -> d e h"))
            const(w2[:, :, :], W2_0.rearrange("e (c p) d -> p (e c) d", c=C0))
            const(v1raw[:, :].rearrange("p (e h) -> p e h", e=E1), W1_1.rearrange("e d h -> d e h"))
            const(v2[:, :, :], W2_1.rearrange("(c q) h d -> (q h) c d", c=NCH))
            for r in range(2):
                const(c2raw[32 * r:32 * r + 32, :], b2_1)
            sp.wait_ge(sem("zeroed"), 1)
            for r in range(2):
                sp.dma_start(b2raw[32 * r:32 * r + 1, :], b2_0.rearrange("(u e) d -> u (e d)", u=1)).then_inc(sem("b2_in"), 16)
                sp.dma_start(selraw[32 * r:32 * r + 32, :].rearrange("e (f h) -> e f h", f=E1),
                             b1_1.rearrange("e (u h) -> e u h", u=1).broadcast_to([E1, E1, H1])).then_inc(sem("b1_in"), 16)

            @each
            def body(j, p):
                g = At(j, p, LAG["A"])
                if g.live():
                    after(sp, "x1", g.before(2))
                    sp.dma_start(x0[g.par][:, :, :], xg[g.n]).then_inc(sem(f"x0_in{g.par}"), 16)
                g = At(j, p, LAG["O"])
                if g.live():
                    after(sp, "fin", g)
                    sp.dma_start(og[g.n], fin[g.par][:, :, :]).then_inc(sem(f"stored{g.par}"), 16)

            body(sp)
            for p in range(2):
                sp.wait_ge(sem(f"stored{p}"), 16 * (NGROUP // 2))

        @block.gpsimd
        def _(pool):
            pool.memset(b2raw[:, :], 0.0)
            pool.memset(neghalf[:, :], -0.5)
            pool.memset(eps[:, :], EPS)
            pool.memset(ident[:, :], 0.0).then_inc(sem("zeroed"), 1)
            pool.wait_ge(sem("zeroed"), 1)
            pool.affine_select(out=ident[:, :], in_=ident[:, :], compare_op=ALU.not_equal, fill=1.0, base=0,
                               pattern=[[-1, P]], channel_multiplier=1).then_inc(sem("ident"), 1)
            pool.iota(iota_i[:, :], pattern=[[1, E1]], base=0, channel_multiplier=0).then_inc(sem("iota"), 1)
            pool.wait_ge(sem("b1_in"), 32)
            pool.wait_ge(sem("masked"), 1)
            for r in range(3):
                if r:
                    pool.wait_ge(sem("sel_raw"), r)
                part = selraw[32 * r:32 * r + 32, :].rearrange("e (f h) -> e f h", f=E1)
                pool.affine_select(out=part, in_=part, compare_op=ALU.is_equal, fill=0.0, base=0,
                                   pattern=[[-1, E1], [0, H1]], channel_multiplier=1).then_inc(sem("sel_raw"), 1)

            def rstd(k, g):
                after(pool, f"moments{k}", g)
                pool.tensor_tensor(ve[k][:, :], mv[k][:, :, 1], eps[:, :], ALU.add).then_inc(sem(f"var_eps{k}"), 1)
                after(pool, f"var_eps{k}", g)
                if k != "C":
                    after(pool, f"xn{k}", g.before(1))
                    pool.tensor_tensor(rs[k][:, :], ve[k][:, :], neghalf[:, :], ALU.pow).then_inc(sem(f"rstd{k}"), 1)
                    return
                c = [v2t[:, n, :] for n in range(4)]
                pool.tensor_tensor(c[0], ve[k][:, :], neghalf[:, :], ALU.pow).then_inc(sem("second"), 1)
                after(pool, "second", g, 5, 1)
                pool.tensor_tensor(c[1], c[0], c[0], ALU.mult).then_inc(sem("second"), 1)
                after(pool, "second", g, 5, 2)
                pool.tensor_tensor(c[2], c[1], mv[k][:, :, 1], ALU.mult).then_inc(sem("second"), 1)
                after(pool, "second", g, 5, 3)
                pool.tensor_tensor(c[1], c[2], eps[:, :], ALU.add).then_inc(sem("second"), 1)
                after(pool, "second", g, 5, 4)
                pool.tensor_tensor(c[3], c[1], neghalf[:, :], ALU.pow).then_inc(sem("second"), 1)
                after(pool, "second", g, 5, 5)
                after(pool, f"xn{k}", g.before(1))
                pool.tensor_tensor(rs[k][:, :], c[0], c[3], ALU.mult).then_inc(sem(f"rstd{k}"), 1)

            @each
            def body(j, p):
                at = {k: At(j, p, lag) for k, lag in LAG.items()}
                for s in range(SLOTS):
                    if s == 0 and at["E"].live():
                        rstd("E", at["E"])
                    if s == 2 and at["C"].live():
                        rstd("C", at["C"])
                    if s == 4 and at["A"].live():
                        rstd("A", at["A"])
                    if s == 5 and at["F"].live():
                        rstd("F", at["F"])
                    g = at["D"]
                    if g.live():
                        after(pool, "ym", g, SLOTS, s + 1)
                        if s == 0:
                            after(pool, "x1", g)
                            prev = x1[g.par]
                        else:
                            after(pool, "ysum", g, SLOTS, s)
                            prev = acc
                        if s == SLOTS - 1:
                            after(pool, "x3", g.before(2))
                        to = x2[g.par] if s == SLOTS - 1 else acc
                        pool.tensor_tensor(to[:, :, :], prev[:, :, :], ym[s % 2][:, :, :], ALU.add).then_inc(sem("ysum"), 1)

            body(pool)

        @block.scalar
        def _(act):
            def xT_out(k, g):
                after(act, f"xn_ps{k}", g)
                if k in "AE":
                    after(act, f"s_ps{k}", g.before(1))
                    act.activation(xnT[k][:, :], TPB[k][:, :], ACT.Copy).then_inc(sem(f"xnT{k}"), 1)
                    return
                scale, bias = (gcol[:, 0:1], bcol[:, 0:1]) if k == "C" else (1.0, 0.0)
                after(act, f"lg_ps{k}", g.before(1))
                after(act, f"xlo{k}", g.before(1))
                act.activation(xnT[k][:, :], TPB[k][:, :], ACT.Identity, scale=scale, bias=bias)
                user = ("d_l1", E0 * C0) if k == "C" else ("m_l1", NCH)
                after(act, user[0], g.before(2), user[1], user[1])
                act.activation(xhi[k][g.par][:, :], TPB[k][:, :], ACT.Identity, scale=scale,
                               bias=bias).then_inc(sem(f"xnT{k}"), 1)

            def h_out(k, g):
                after(act, f"h_ps{k}", g)
                after(act, f"att_ps{'B' if k == 'A' else 'F'}", g.before(2))
                act.activation(hg[k][g.par][:, :, :], g4(HB), ACT.Copy).then_inc(sem(f"h{k}"), 1)
                after(act, f"s_ps{k}", g)
                after(act, f"raw{k}", g.before(1))
                act.activation(s1[k][:, :], TPB[k][:, 0:G], ACT.Copy).then_inc(sem(f"s1{k}"), 1)

            def prT_out(k, g):
                after(act, f"pr_ps{k}", g)
                after(act, f"att_ps{k}", g.before(1))
                act.activation(prT[k][:, :], TPB[k][:, :], ACT.Copy).then_inc(sem(f"prT{k}"), 1)

            def exps(at):
                for k, src in (("F", "E"), ("B", "A")):
                    g = at[k]
                    if g.live():
                        after(act, f"score{src}", g)
                        after(act, f"pr_ps{k}", g.before(1))
                        after(act, f"rsum{k}", g.before(1))
                        act.activation(pr[k][:, :, :], sc[src][:, :, :], ACT.Exp).then_inc(sem(f"pr{k}"), 1)
                g = at["C"]
                if g.live():
                    after(act, "zneg", g)
                    after(act, "x1", g.before(1))
                    act.activation(eneg[:, :, :], zneg[:, :, :], ACT.Exp).then_inc(sem("eneg"), 1)

            @each
            def body(j, p):
                at = {k: At(j, p, lag) for k, lag in LAG.items()}
                for s in range(SLOTS):
                    g = at["D"]
                    if g.live():
                        for c in range(C0):
                            n = C0 * s + c
                            after(act, "d_l1", g, E0 * C0, n + 1)
                            if s >= 2:
                                after(act, "d_l2", g, E0, s - 1)
                            else:
                                after(act, "d_l2", g.before(1), E0, E0 + s - 1)
                            act.activation(hid[s % 2][c][:, :], ZB[(3 * s + c) % 2][:, :], ACT.Gelu,
                                           bias=b1col[:, n:n + 1]).then_inc(sem("gelu"), 1)
                    g = at["M"]
                    if g.live():
                        after(act, "m_l1", g, NCH, s + 1)
                        if s >= 2:
                            after(act, "m_l2", g, NCH, s - 1)
                        else:
                            after(act, "m_l2", g.before(1), NCH, NCH + s - 1)
                        act.activation(rel[s % 2][:, :], ZB[(3 * s + 2) % 2][:, :], ACT.Relu).then_inc(sem("relu"), 1)
                    if s == 0:
                        exps(at)
                    if s == 1 and at["E"].live():
                        xT_out("E", at["E"])
                    if s == 2:
                        if at["E"].live():
                            h_out("E", at["E"])
                        if at["B"].live():
                            prT_out("B", at["B"])
                    if s == 3 and at["F"].live():
                        prT_out("F", at["F"])
                    if s == 4 and at["C"].live():
                        xT_out("C", at["C"])
                    if s == 5 and at["A"].live():
                        xT_out("A", at["A"])
                    if s == 6:
                        if at["F"].live():
                            xT_out("F", at["F"])
                        if at["C"].live():
                            after(act, "dif", at["C"])
                            act.activation(th[:, :], dif[:, :], ACT.Tanh, scale=0.5).then_inc(sem("tanh"), 1)
                        if at["A"].live():
                            h_out("A", at["A"])
                    if s == 7:
                        g = at["F"]
                        if g.live():
                            after(act, "oh_ps", g)
                            after(act, "m_l2", g.before(2), NCH, NCH)
                            act.activation(ohT[g.par][:, :], TP1[0:3 * E1, :], ACT.Copy).then_inc(sem("ohT"), 1)
                        g = at["M"]
                        if g.live():
                            after(act, "m_l2", g, NCH, NCH)
                            after(act, "out_ps", g.before(1))
                            act.activation(oT[:, :], OB[:, :], ACT.Relu).then_inc(sem("oT"), 1)

            body(act)

        @block.vector
        def _(dve):
            steps = [0]

            def link(ins):
                steps[0] += 1
                ins.then_inc(sem("setup_v"), 1)
                dve.wait_ge(sem("setup_v"), steps[0])

            dve.memset(selraw[64:96, :], MASKED).then_inc(sem("masked"), 1)
            dve.memset(ones[:, :], 1.0)
            dve.memset(ones_r[:, :].bitcast(F32), 1.0)
            dve.wait_ge(sem("const_in"), 16 * NCONST)
            dve.tensor_copy(adj_f[:, :], adj_i[:, :])
            dve.tensor_copy(w1hi[:, :], w1raw[:, :])
            dve.tensor_copy(v1hi[:, :], v1raw[:, :])
            dve.tensor_copy(c2hi[:, :], c2raw[:, :])
            link(dve.tensor_tensor(wprod[:, 0, :, :], Wg[0][:, :].unsqueeze(1).broadcast_to([P, 2, P]), arow[:, 0, :, :], ALU.mult))
            link(dve.tensor_tensor(wprod[:, 1, :, :], Wg[1][:, :].unsqueeze(1).broadcast_to([P, 2, P]), arow[:, 1, :, :], ALU.mult))
            dve.tensor_tensor(w1lo[:, :], w1raw[:, :], w1hi[:, :].bitcast(F32), ALU.subtract)
            dve.tensor_tensor(v1lo[:, :], v1raw[:, :], v1hi[:, :].bitcast(F32), ALU.subtract)
            dve.tensor_copy(c2[0:32, :], c2hi[0:32, :].bitcast(F32))
            dve.tensor_tensor(c2[32:64, :], c2raw[32:64, :], c2hi[32:64, :].bitcast(F32), ALU.subtract)
            dve.tensor_scalar(adj_m[:, 0, :], adj_f[:, :], 0.0, 1.0, ALU.is_gt, ALU.subtract)
            link(dve.tensor_scalar(adj_m[:, 1, :], adj_f[:, :], 0.0, 1.0, ALU.not_equal, ALU.subtract))
            for l in range(2):
                dve.tensor_scalar(mask[l][:, :], adj_m[:, l, :], -MASKED, None, ALU.mult)
            link(dve.reduce_sum(wa[:, :, :], wprod[:, :, :, :], AX.X))
            for l in range(2):
                dve.tensor_scalar(wa2rep[l][:, :], ones[:, :], wa[:, l, 1:2], None, ALU.mult)
            dve.wait_ge(sem("ident"), 1)
            dve.tensor_copy(identb[:, :], ident[:, :])
            dve.wait_ge(sem("iota"), 1)
            dve.tensor_copy(iota[:, :], iota_i[:, :])
            dve.wait_ge(sem("b2_in"), 32)
            dve.wait_ge(sem("zeroed"), 1)
            link(dve.tensor_copy(b2hi[:, :], b2raw[:, :]))
            dve.tensor_copy(b2c[0:32, :], b2hi[0:32, :].bitcast(F32))
            dve.tensor_tensor(b2c[32:64, :], b2raw[32:64, :], b2hi[32:64, :].bitcast(F32), ALU.subtract)
            dve.wait_ge(sem("sel_raw"), 3)
            link(dve.tensor_copy(selhi[:, :], selraw[:, :]))
            dve.tensor_copy(sel[0:32, :], selhi[0:32, :].bitcast(F32))
            dve.tensor_tensor(sel[32:64, :], selraw[32:64, :], selhi[32:64, :].bitcast(F32), ALU.subtract)
            dve.tensor_copy(sel[64:96, :], selhi[64:96, :].bitcast(F32)).then_inc(sem("consts"), 1)
            dve.wait_ge(sem("cols_ps"), 1)
            dve.tensor_copy(rwT[:, :], TP0[:, 0:E1])
            dve.tensor_copy(b1col[:, :], TP0[:, E1:E1 + E0 * C0]).then_inc(sem("cols"), 1)
            dve.wait_ge(sem("cols"), 1)

            def stats(k, g, xin):
                for n in range(G):
                    last = dve.bn_stats(st[k][:, n, :], xin[:, n, :])
                last.then_inc(sem(f"stats{k}"), 1)
                after(dve, f"stats{k}", g)
                after(dve, f"rstd{k}", g.before(1))
                settle()
                for n in range(G):
                    last = dve.bn_aggr(mv[k][:, n, :], st[k][:, n, :])
                last.then_inc(sem(f"moments{k}"), 1)

            def norm(k, g, xin):
                after(dve, f"rstd{k}", g)
                after(dve, f"xn_ps{k}", g.before(1))
                for n in range(G):
                    last = dve.tensor_scalar(xn[k][:, n, :], xin[:, n, :], mv[k][:, n, 0:1], rs[k][:, n:n + 1],
                                             ALU.subtract, ALU.mult)
                last.then_inc(sem(f"xn{k}"), 1)

            def scores(k, g):
                l = "AE".index(k)
                after(dve, f"s1{k}", g)
                dve.tensor_tensor(tt[k][:, :, :], g4(SB), s1[k][:, :].unsqueeze(2).broadcast_to([P, G, P]),
                                  ALU.add).then_inc(sem(f"raw{k}"), 1)
                after(dve, f"raw{k}", g)
                dve.scalar_tensor_tensor(ee[k][:, :, :], tt[k][:, :, :], SLOPE[l], tt[k][:, :, :], ALU.mult,
                                         ALU.max).then_inc(sem(f"leaky{k}"), 1)
                after(dve, f"leaky{k}", g)
                dve.reduce_max(em[k][:, :], ee[k][:, :, :], AX.X).then_inc(sem(f"rowmax{k}"), 1)
                after(dve, f"rowmax{k}", g)
                after(dve, f"pr{'B' if k == 'A' else 'F'}", g.before(1))
                dve.tensor_tensor(sc[k][:, :, :], ee[k][:, :, :], em[k][:, :].unsqueeze(2).broadcast_to([P, G, P]),
                                  ALU.subtract).then_inc(sem(f"score{k}"), 1)

            def row_sums(k, g):
                after(dve, f"pr{k}", g)
                dve.reduce_sum(rsum[k][:, :], pr[k][:, :, :], AX.X).then_inc(sem(f"rsum{k}"), 1)
                after(dve, f"rsum{k}", g)
                after(dve, f"z{k}", g.before(1))
                dve.reciprocal(rinv[k][:, :], rsum[k][:, :]).then_inc(sem(f"rinv{k}"), 1)

            def attended(k, g):
                after(dve, f"rinv{k}", g)
                after(dve, f"att_ps{k}", g)
                if k == "B":
                    after(dve, "x1a", g.before(1))
                dve.tensor_tensor(z[k][:, :, :], g4(HB), rinv[k][:, :].unsqueeze(2).broadcast_to([P, G, P]),
                                  ALU.mult).then_inc(sem(f"z{k}"), 1)
                after(dve, f"z{k}", g)

            def logits(k, g, bias, n):
                after(dve, f"lg_ps{k}", g)
                dve.tensor_tensor(lg[k][:, :, :], SB[:, 0:G * n].rearrange("p (g e) -> p g e", g=G),
                                  bias[:, :].unsqueeze(1).broadcast_to([P, G, n]), ALU.add).then_inc(sem(f"lg{k}"), 1)
                after(dve, f"lg{k}", g)
                settle()
                for q in range(G):
                    last = dve.max(top[k][:, q, :], lg[k][:, q, :])
                last.then_inc(sem(f"top{k}"), 1)
                after(dve, f"top{k}", g)
                settle()
                for q in range(G):
                    last = dve.max_index(idx[k][:, q, :], top[k][:, q, :], lg[k][:, q, :])
                last.then_inc(sem(f"idx{k}"), 1)
                after(dve, f"idx{k}", g)
                dve.tensor_copy(idf[k][:, :, :], idx[k][:, :, 0:2]).then_inc(sem(f"idf{k}"), 1)

            @each
            def body(j, p):
                at = {k: At(j, p, lag) for k, lag in LAG.items()}
                A, B, C, D, E, F, M, O = (at[k] for k in "ABCDEFMO")
                for s in range(SLOTS):
                    if s == 0 and E.live():
                        after(dve, "ysum", E, SLOTS, SLOTS)
                        stats("E", E, x2[E.par])
                    if s == 2 and C.live():
                        norm("C", C, x1[C.par])
                    if s == 4 and A.live():
                        norm("A", A, x0[A.par])
                    if s == 5 and F.live():
                        norm("F", F, x3[F.par])
                    if D.live():
                        after(dve, "d_l2", D, E0, s + 1)
                        if s >= 2:
                            after(dve, "ysum", D, SLOTS, s - 1)
                        else:
                            after(dve, "ysum", D.before(1), SLOTS, SLOTS + s - 1)
                        dve.tensor_tensor(ym[s % 2][:, :, :], g4(YB), wgt[D.par][:, :, s:s + 1].broadcast_to([P, G, P]),
                                          ALU.mult).then_inc(sem("ym"), 1)
                    if s == 0:
                        if E.live():
                            norm("E", E, x2[E.par])
                        if O.live():
                            after(dve, "out_ps", O)
                            if O.before(2).live():
                                dve.wait_ge(sem(f"stored{O.par}"), 16 * (O.half))
                            dve.tensor_tensor(fin[O.par][:, :, :], g4(TP1), x3[O.par][:, :, :], ALU.add).then_inc(sem("fin"), 1)
                    if s == 1 and C.live():
                        dve.scalar_tensor_tensor(x1a[:, :, :], z["B"][:, :, :], 0.0, x0[C.par][:, :, :], ALU.max,
                                                 ALU.add).then_inc(sem("x1a"), 1)
                        after(dve, "x1a", C)
                        after(dve, "eneg", C)
                        dve.scalar_tensor_tensor(x1[C.par][:, :, :], eneg[:, :, :], 1.0, x1a[:, :, :], ALU.subtract,
                                                 ALU.add).then_inc(sem("x1"), 1)
                        after(dve, "x1", C)
                        stats("C", C, x1[C.par])
                    if s == 1 and B.live():
                        row_sums("B", B)
                    if s == 1 and F.live():
                        row_sums("F", F)
                    if s == 2 and E.live():
                        scores("E", E)
                    if s == 3:
                        if B.live():
                            attended("B", B)
                            after(dve, "eneg", B.before(1))
                            dve.tensor_scalar(zneg[:, :, :], z["B"][:, :, :], 0.0, None, ALU.min).then_inc(sem("zneg"), 1)
                        if A.live():
                            dve.wait_ge(sem(f"x0_in{A.par}"), 16 * (A.half + 1))
                            stats("A", A, x0[A.par])
                    if s == 4:
                        if F.live():
                            attended("F", F)
                            after(dve, "fin", F.before(2))
                            dve.scalar_tensor_tensor(x3[F.par][:, :, :], z["F"][:, :, :], 0.0, x2[F.par][:, :, :], ALU.max,
                                                     ALU.add).then_inc(sem("x3"), 1)
                            after(dve, "x3", F)
                            stats("F", F, x3[F.par])
                        if C.live():
                            after(dve, "xnTC", C)
                            after(dve, "d_l1", C.before(2), E0 * C0, E0 * C0)
                            dve.tensor_tensor(xlo["C"][C.par][:, :], xnT["C"][:, :], xhi["C"][C.par][:, :].bitcast(F32),
                                              ALU.subtract).then_inc(sem("xloC"), 1)
                    if s == 5 and C.live():
                        logits("C", C, brow, E0)
                        after(dve, "tanh", C.before(1))
                        dve.tensor_tensor(dif[:, :], top["C"][:, :, 0], top["C"][:, :, 1], ALU.subtract).then_inc(sem("dif"), 1)
                        after(dve, "idfC", C)
                        for n in range(2):
                            dve.tensor_tensor(oh2[:, n, :, :], iota[:, 0:E0].unsqueeze(1).broadcast_to([P, G, E0]),
                                              idf["C"][:, :, n:n + 1].broadcast_to([P, G, E0]),
                                              ALU.is_equal).then_inc(sem("oh2"), 1)
                    if s == 6:
                        if C.live():
                            after(dve, "tanh", C)
                            dve.tensor_scalar(w01[:, 0, :], th[:, :], 0.5, 0.5, ALU.mult, ALU.add)
                            dve.tensor_scalar(w01[:, 1, :], th[:, :], -0.5, 0.5, ALU.mult, ALU.add).then_inc(sem("w01"), 1)
                            after(dve, "w01", C)
                            after(dve, "oh2", C, 2, 2)
                            dve.tensor_tensor(ohw[:, :, :, :], oh2[:, :, :, :],
                                              w01[:, :, :].unsqueeze(3).broadcast_to([P, 2, G, E0]),
                                              ALU.mult).then_inc(sem("ohw"), 1)
                            after(dve, "ohw", C)
                            dve.tensor_tensor(wgt[C.par][:, :, :], ohw[:, 0, :, :], ohw[:, 1, :, :], ALU.add).then_inc(sem("wgt"), 1)
                            after(dve, "wgt", C)
                        if A.live():
                            scores("A", A)
                        if F.live():
                            after(dve, "xnTF", F)
                            after(dve, "m_l1", F.before(2), NCH, NCH)
                            dve.tensor_tensor(xlo["F"][F.par][:, :], xnT["F"][:, :], xhi["F"][F.par][:, :].bitcast(F32),
                                              ALU.subtract).then_inc(sem("xloF"), 1)
                            logits("F", F, rbrow, E1)
                            after(dve, "idfF", F)
                            after(dve, "oh_ps", F.before(1))
                            for r in range(3):
                                op = ALU.not_equal if r == 2 else ALU.is_equal
                                last = dve.tensor_tensor(ohc[:, :, r * E1:(r + 1) * E1],
                                                         iota[:, :].unsqueeze(1).broadcast_to([P, G, E1]),
                                                         idf["F"][:, :, 0:1].broadcast_to([P, G, E1]), op)
                            last.then_inc(sem("ohc"), 1)

            body(dve)

        @block.tensor
        def _(pe):
            pe.wait_ge(sem("ident"), 1)
            pe.wait_ge(sem("const_in"), 16 * NCONST)
            pe.transpose(TP0[:, 0:E1], rw_row[:, :], ident[0:E1, 0:E1])
            pe.transpose(TP0[:, E1:E1 + E0 * C0], b1row[:, :], ident[0:E0 * C0, 0:E0 * C0]).then_inc(sem("cols_ps"), 1)
            pe.wait_ge(sem("consts"), 1)
            pe.wait_ge(sem("cols"), 1)

            def turn(bank, src, done, n=P):
                for q in range(G):
                    last = pe.transpose(bank[0:n, q * P:(q + 1) * P], src[:, q, :], ident[:, :])
                last.then_inc(sem(done), 1)

            def rows(k, g):
                after(pe, f"xn{k}", g)
                turn(TPB[k], xn[k], f"xn_ps{k}")

            def front(k, g):
                l = "AE".index(k)
                after(pe, f"xnT{k}", g)
                for q in range(G):
                    last = pe.matmul(HB[:, q * P:(q + 1) * P], xnT[k][:, q * P:(q + 1) * P], Wg[l][:, :],
                                     start=(q == 0), stop=(q == G - 1), skip_group_check=True)
                last.then_inc(sem(f"h_ps{k}"), 1)
                pe.matmul(SB[:, :], wa2rep[l][:, :], xnT[k][:, :], start=True, stop=False)
                pe.matmul(g4(SB), identb[:, :], mask[l][:, :].unsqueeze(1).broadcast_to([P, G, P]), start=False, stop=True)
                for q in range(G):
                    last = pe.matmul(TPB[k][:, q:q + 1], xnT[k][:, q * P:(q + 1) * P], wa[:, l, 0:1],
                                     start=(q == 0), stop=(q == G - 1), skip_group_check=True)
                last.then_inc(sem(f"s_ps{k}"), 1)

            def attend(k, src, g):
                after(pe, f"prT{k}", g)
                for q in range(G):
                    last = pe.matmul(HB[:, q * P:(q + 1) * P], prT[k][:, q * P:(q + 1) * P], hg[src][g.par][:, q, :],
                                     start=(q == 0), stop=(q == G - 1), skip_group_check=True)
                last.then_inc(sem(f"att_ps{k}"), 1)

            def route(k, g, w, n):
                after(pe, f"xnT{k}", g)
                for q in range(G):
                    last = pe.matmul(SB[:, q * n:(q + 1) * n], xnT[k][:, q * P:(q + 1) * P], w[:, :],
                                     start=(q == 0), stop=(q == G - 1), skip_group_check=True)
                last.then_inc(sem(f"lg_ps{k}"), 1)

            @each
            def body(j, p):
                at = {k: At(j, p, lag) for k, lag in LAG.items()}
                A, B, C, D, E, F, M, O = (at[k] for k in "ABCDEFMO")

                def split(out_, w_hi, w_lo, k, g, stop, done):
                    hi, lo = xhi[k][g.par], xlo[k][g.par]
                    pe.matmul(out_[:, :], w_hi, hi[:, :], start=True, stop=False)
                    pe.matmul(out_[:, :], w_lo, hi[:, :], start=False, stop=False)
                    last = pe.matmul(out_[:, :], w_hi, lo[:, :], start=False, stop=stop)
                    if stop:
                        last.then_inc(sem(done), 1)

                def z_free(u):
                    v, prev = u - 2, 0
                    if v < 0:
                        v, prev = v + 3 * SLOTS, 1
                    s, c = divmod(v, 3)
                    if c == 2:
                        after(pe, "relu", M.before(prev), NCH, s + 1)
                    else:
                        after(pe, "gelu", D.before(prev), E0 * C0, C0 * s + c + 1)

                for s in range(SLOTS):
                    if D.live():
                        if s == 0:
                            after(pe, "xloC", D)
                        for c in range(C0):
                            n = C0 * s + c
                            z_free(3 * s + c)
                            w = slice(n * P, (n + 1) * P)
                            split(ZB[(3 * s + c) % 2], w1hi[:, w], w1lo[:, w], "C", D, True, "d_l1")
                    if M.live():
                        if s == 0:
                            after(pe, "xloF", M)
                            after(pe, "ohT", M)
                        z_free(3 * s + 2)
                        w = slice(s * P, (s + 1) * P)
                        zb = ZB[(3 * s + 2) % 2]
                        split(zb, v1hi[:, w], v1lo[:, w], "F", M, False, None)
                        pe.matmul(zb[:, :], sel[:, w], ohT[M.par][:, :], start=False, stop=True).then_inc(sem("m_l1"), 1)
                    if s == 0 and O.live():
                        after(pe, "oT", O)
                        after(pe, "ohT", F.before(1))
                        after(pe, "fin", O.before(1))
                        for q in range(G):
                            last = pe.transpose(TP1[:, q * P:(q + 1) * P], oT[:, q * P:(q + 1) * P], ident[:, :])
                        last.then_inc(sem("out_ps"), 1)
                    if s == 1 and E.live():
                        after(pe, "fin", O)
                        after(pe, "ohT", F.before(1))
                        rows("E", E)
                    if s == 2:
                        if E.live():
                            after(pe, "zF", F.before(1))
                            after(pe, "hA", A.before(1))
                            after(pe, "rawA", A.before(1))
                            after(pe, "lgF", F.before(1))
                            front("E", E)
                        if B.live():
                            after(pe, "s1A", A.before(1))
                            after(pe, "prB", B)
                            turn(TP0, pr["B"], "pr_psB")
                    if s == 3:
                        if F.live():
                            after(pe, "s1E", E)
                            after(pe, "fin", O)
                            after(pe, "ohT", F.before(1))
                            after(pe, "prF", F)
                            turn(TP1, pr["F"], "pr_psF")
                        if B.live():
                            after(pe, "hE", E)
                            after(pe, "hA", A.before(1))
                            after(pe, "zF", F.before(1))
                            attend("B", "A", B)
                    if s == 4:
                        if F.live():
                            after(pe, "zB", B)
                            after(pe, "hE", E)
                            after(pe, "zF", F.before(1))
                            attend("F", "E", F)
                        if C.live():
                            after(pe, "prTB", B)
                            after(pe, "s1A", A.before(1))
                            after(pe, "xnTC", C.before(1))
                            rows("C", C)
                    if s == 5:
                        if C.live():
                            after(pe, "rawE", E)
                            after(pe, "rawA", A.before(1))
                            after(pe, "lgF", F.before(1))
                            route("C", C, wr_sb, E0)
                        if A.live():
                            after(pe, "xnTC", C)
                            after(pe, "prTB", B)
                            after(pe, "s1A", A.before(1))
                            rows("A", A)
                    if s == 6:
                        if A.live():
                            after(pe, "zF", F)
                            after(pe, "zB", B)
                            after(pe, "hE", E)
                            after(pe, "lgC", C)
                            after(pe, "rawE", E)
                            front("A", A)
                        if F.live():
                            after(pe, "prTF", F)
                            after(pe, "s1E", E)
                            rows("F", F)
                    if D.live():
                        if s == 0:
                            after(pe, "ym", D.before(1), E0, E0)
                            after(pe, "wgt", D)
                        else:
                            after(pe, "ym", D, E0, s)
                        pe.matmul(g4(YB), ones_r[:, :], b2c[:, s * P:(s + 1) * P].unsqueeze(1).broadcast_to([64, G, P]),
                                  start=True, stop=False, skip_group_check=True)
                        for c in range(C0):
                            after(pe, "gelu", D, E0 * C0, C0 * s + c + 1)
                            for q in range(G):
                                last = pe.matmul(YB[:, q * P:(q + 1) * P], hid[s % 2][c][:, q * P:(q + 1) * P],
                                                 w2[:, C0 * s + c, :], start=False, stop=(c == C0 - 1),
                                                 skip_group_check=True)
                        last.then_inc(sem("d_l2"), 1)
                    if s == 6 and F.live():
                        after(pe, "rawA", A)
                        after(pe, "lgC", C)
                        after(pe, "rawE", E)
                        after(pe, "lgF", F.before(1))
                        route("F", F, rwT, E1)
                    if s == 7 and F.live():
                        after(pe, "ohc", F)
                        after(pe, "xnTF", F)
                        turn(TP1, ohc, "oh_ps", 3 * E1)
                    if M.live():
                        if s == 0:
                            after(pe, "oT", M.before(1))
                        after(pe, "relu", M, NCH, s + 1)
                        last = pe.matmul(OB[:, :], v2[:, s, :], rel[s % 2][:, :], start=(s == 0), stop=False)
                        if s == NCH - 1:
                            last = pe.matmul(OB[:, :], c2[:, :], ohT[M.par][0:2 * E1, :], start=False, stop=True)
                        last.then_inc(sem("m_l2"), 1)

            body(pe)


_INS = ["x", "adj", "L0_gnn_W", "L0_gnn_a", "L0_ffn_gamma", "L0_ffn_beta", "L0_ffn_Wr", "L0_ffn_br", "L0_ffn_W1",
        "L0_ffn_b1", "L0_ffn_W2", "L0_ffn_b2", "L1_gnn_W", "L1_gnn_a", "L1_ffn_router_w", "L1_ffn_router_b",
        "L1_ffn_W1", "L1_ffn_b1", "L1_ffn_W2", "L1_ffn_b2"]


def kernel(**inputs):
    import numpy as np
    import concourse.bacc as bacc
    from concourse.bass_utils import run_bass_kernel_spmd

    nc = bacc.Bacc("TRN2", target_bir_lowering=False, num_devices=1)
    arrays, args = {}, []
    for name in _INS:
        a = np.ascontiguousarray(inputs[name])
        arrays[f"in_{name}"] = a
        args.append(nc.dram_tensor(f"in_{name}", a.shape, mybir.dt.from_np(a.dtype), kind="ExternalInput").ap())
    o = nc.dram_tensor("out", [NGRAPH, P, P], F32, kind="ExternalOutput").ap()
    program(nc, *args, o)
    r = run_bass_kernel_spmd(nc, [arrays], core_ids=[0])
    return r.results[0]["out"]
```

```python
from contextlib import ExitStack

import concourse.bass as bass
from concourse import mybir

F32 = mybir.dt.float32
F32R = mybir.dt.float32r
BF16 = mybir.dt.bfloat16
I32 = mybir.dt.int32
U32 = mybir.dt.uint32
ALU = mybir.AluOpType
ACT = mybir.ActivationFunctionType
AX = mybir.AxisListType

P = 128
NGRAPH = 128
G = 4
T = G * P
NGROUP = NGRAPH // G
E0, H0 = 8, 256
C0 = H0 // P
E1, H1 = 32, 32
NCH = E1 * H1 // P
SLOTS = 8
assert E0 == SLOTS and NCH == SLOTS
EPS = 1e-5
SLOPE = (0.2, 0.01)
MASKED = -1e30

LAG = dict(A=0, a=1, B=2, C=3, D=4, E=5, e=6, F=7, M=8, O=9)
NITER = NGROUP + LAG["O"]
NTURN = NGROUP + LAG["F"] - LAG["C"]
FIRST = 12


class At:

    def __init__(self, j, p, lag, total=NGROUP):
        self.j, self.p, self.lag, self.total = j, p, lag, total
        self.n = 2 * j + (p - lag)
        self.fixed = isinstance(j, int)

    @property
    def par(self):
        return (self.p - self.lag) % 2

    @property
    def half(self):
        return self.j + (self.p - self.lag) // 2

    def live(self):
        return not self.fixed or 0 <= self.n < self.total

    def before(self, k):
        return At(self.j, self.p, self.lag + k, self.total)

    def count(self, per, k):
        if not self.fixed:
            return per * self.n + k
        if self.n < 0:
            return None
        return per * self.total if self.n >= self.total else per * self.n + k


def stages(j, p):
    at = {k: At(j, p, lag) for k, lag in LAG.items()}
    at["W"] = At(j, p, LAG["C"], NTURN)
    return at


def program(nc, x, adj, W_0, a_0, gamma, beta, Wr, br, W1_0, b1_0, W2_0, b2_0,
            W_1, a_1, rw, rb, W1_1, b1_1, W2_1, b2_1, out):
    ctx = ExitStack()
    with ctx:
        def sb(name, shape, dt=F32):
            return ctx.enter_context(nc.sbuf_tensor(name, shape, dt))

        def pb(name):
            return ctx.enter_context(nc.psum_tensor(name, [P, T], F32))

        sems = {}

        def sem(name):
            if name not in sems:
                sems[name] = ctx.enter_context(nc.semaphore(name))
            return sems[name]

        def after(eng, name, g, per=1, k=1):
            v = g.count(per, k)
            if v is not None:
                eng.wait_ge(sem(name), v)

        def settle():
            nc.vector.memset(spare[:, :], 0.0)

        WHI, WLO = 3 * E1, 3 * E1 + E0
        ident = sb("ident", [P, P])
        identb = sb("identb", [P, P], BF16)
        mask = [sb(f"mask{l}", [P, P], BF16) for l in range(2)]
        Wg = [sb(f"Wg{l}", [P, P + 1]) for l in range(2)]
        wa = sb("wa", [P, 2, 2])
        ones = sb("ones", [P, P])
        wa2rep = [sb(f"wa2rep{l}", [P, P]) for l in range(2)]
        gcol = sb("gcol", [P, 1])
        bcol = sb("bcol", [P, 1])
        b1col = sb("b1col", [P, E0 * C0])
        b1row = sb("b1row", [E0 * C0, P])
        wr_sb = sb("wr_sb", [P, E0])
        brow = sb("brow", [P, E0])
        rw_row = sb("rw_row", [E1, P])
        rwT = sb("rwT", [P, E1])
        rbrow = sb("rbrow", [P, E1])
        iota_i = sb("iota_i", [P, E1], I32)
        iota = sb("iota", [P, E1])
        spare = sb("spare", [P, 1])
        eps = sb("eps", [P, G])
        neghalf = sb("neghalf", [P, G])
        w1hi = sb("w1hi", [P, E0 * H0], F32R)
        w1lo = sb("w1lo", [P, E0 * H0], F32R)
        w2hi = sb("w2hi", [P, E0 * C0, P], F32R)
        w2lo = sb("w2lo", [P, E0 * C0, P], F32R)
        b2col = sb("b2col", [P, E0])
        b2row = sb("b2row", [E0, P])
        spread = sb("spread", [P, E0 * P], F32R)
        v1hi = sb("v1hi", [P, E1 * H1], F32R)
        v1lo = sb("v1lo", [P, E1 * H1], F32R)
        v2hi = sb("v2hi", [P, NCH, P], F32R)
        v2lo = sb("v2lo", [P, NCH, P], F32R)
        c2 = sb("c2", [64, P], F32R)
        sel = sb("sel", [P, E1 * H1], F32R)

        x0 = [sb(f"x0_{p}", [P, G, P]) for p in range(2)]
        x0k = [sb(f"x0k_{p}", [P, G, P]) for p in range(2)]
        x1 = [sb(f"x1_{p}", [P, G, P]) for p in range(2)]
        x2 = [sb(f"x2_{p}", [P, G, P]) for p in range(2)]
        x3 = [sb(f"x3_{p}", [P, G, P]) for p in range(2)]
        st = {k: sb(f"st{k}", [P, G, 6]) for k in "ACEF"}
        mv = {k: sb(f"mv{k}", [P, G, 2]) for k in "ACEF"}
        ve = {k: sb(f"ve{k}", [P, G]) for k in "ACEF"}
        rs = {k: sb(f"rs{k}", [P, G]) for k in "ACEF"}
        v2t = sb("v2t", [P, 4, G])
        xn = {k: sb(f"xn{k}", [P, G, P]) for k in "AE"}
        xn["C"], xn["F"] = xn["A"], xn["E"]
        xnT = {k: sb(f"xnT{k}", [P, T]) for k in "ACEF"}
        hg = {k: [sb(f"hg{k}{p}", [P, G, P]) for p in range(2)] for k in "AE"}
        s1 = {k: sb(f"s1{k}", [P, G]) for k in "AE"}
        tt = {k: sb(f"tt{k}", [P, G, P]) for k in "AE"}
        em = {k: sb(f"em{k}", [P, G]) for k in "AE"}
        sc = {k: sb(f"sc{k}", [P, G, P]) for k in "AE"}
        pr = {k: sb(f"pr{k}", [P, G, P]) for k in "BF"}
        rsum = {k: sb(f"rsum{k}", [P, G]) for k in "BF"}
        rinv = {k: sb(f"rinv{k}", [P, G]) for k in "BF"}
        z = {k: sb(f"z{k}", [P, G, P]) for k in "BF"}
        zneg = sb("zneg", [P, G, P])
        xhi = {k: [sb(f"xhi{k}{p}", [P, T], F32R) for p in range(2)] for k in "CF"}
        xlo = {k: [sb(f"xlo{k}{p}", [P, T], F32R) for p in range(2)] for k in "CF"}
        lg = {"C": sb("lgC", [P, G, E0]), "F": sb("lgF", [P, G, E1])}
        top = {k: sb(f"top{k}", [P, G, 8]) for k in "CF"}
        idx = {k: sb(f"idx{k}", [P, G, 8], U32) for k in "CF"}
        idf = {k: sb(f"idf{k}", [P, G, 2]) for k in "CF"}
        dif = sb("dif", [P, G])
        th = sb("th", [P, G])
        w01 = sb("w01", [P, 2, G])
        oh2 = sb("oh2", [P, 2, G, E0])
        ohw = sb("ohw", [P, 2, G, E0])
        wgt = sb("wgt", [P, G, E0])
        wb = [sb(f"wb{s}", [P, T]) for s in range(2)]
        x1n = sb("x1n", [P, G, P])
        wo = sb("wo", [P, G, P])
        woT = [sb(f"woT{p}", [P, T], F32R) for p in range(2)]
        with ExitStack() as early:
            def raw(name, shape, dt=F32):
                return early.enter_context(nc.sbuf_tensor(name, shape, dt))

            w1raw = raw("w1raw", [P, E0 * H0])
            w2raw = raw("w2raw", [P, E0 * C0, P])
            v1raw = raw("v1raw", [P, E1 * H1])
            v2raw = raw("v2raw", [P, NCH, P])
            spread_f = raw("spread_f", [P, E0 * P])
            c2raw = raw("c2raw", [64, P])
            c2hi = raw("c2hi", [64, P], F32R)
            selraw = raw("selraw", [P, E1 * H1])
            selhi = raw("selhi", [P, E1 * H1], F32R)
            arow = raw("arow", [P, 2, 2, P])
            wprod = raw("wprod", [P, 2, 2, P])
            adj_i = raw("adj_i", [P, P], I32)
            adj_f = raw("adj_f", [P, P])
            adj_m = raw("adj_m", [P, 2, P])
        prT = {k: sb(f"prT{k}", [P, T]) for k in "BF"}
        fin = [sb(f"fin{p}", [P, G, P]) for p in range(2)]
        hid = [[sb(f"hid{s}{c}", [P, T]) for c in range(C0)] for s in range(2)]
        hhi = [[sb(f"hhi{s}{c}", [P, T], F32R) for c in range(C0)] for s in range(2)]
        hlo = [[sb(f"hlo{s}{c}", [P, T], F32R) for c in range(C0)] for s in range(2)]
        rhi = [sb(f"rhi{s}", [P, T], F32R) for s in range(2)]
        rlo = [sb(f"rlo{s}", [P, T], F32R) for s in range(2)]
        ym = [sb(f"ym{s}", [P, T]) for s in range(2)]
        acc = [sb(f"acc{p}", [P, T]) for p in range(2)]
        oT = sb("oT", [P, T])

        ZB = [pb("Z0"), pb("Z1")]
        YB = pb("Y")
        OB = pb("O")
        TP0 = pb("TP0")
        TP1 = pb("TP1")
        HB = pb("H")
        SB = pb("S")
        TPB = dict(A=TP0, B=TP0, C=TP0, E=TP1, F=TP1)

        def g4(t):
            return t[:, :].rearrange("p (g f) -> p g f", g=G)

        def each(body):
            def run(eng, *a):
                for i in range(FIRST):
                    body(i // 2, i % 2)
                with eng.Fori(FIRST // 2, NGROUP // 2) as j:
                    for p in range(2):
                        body(j, p)
                for i in range(NGROUP, NITER):
                    body(i // 2, i % 2)
            return run

        def h3(k):
            return (HB if k == "A" else TP1)[:, 0:(G - 1) * (P + 1)].rearrange("p (g f) -> p g f", g=G - 1)

        def h4(k):
            n = "AE".index(k) * (P + 1)
            return TP0[:, n:n + P + 1]

        def l2_done(eng, g, s):
            if s >= 2:
                after(eng, "d_l2", g, E0, s - 1)
            else:
                after(eng, "d_l2", g.before(1), E0, E0 + s - 1)

        def m2_done(eng, g, s):
            if s >= 2:
                after(eng, "m_l2", g, NCH, s - 1)
            else:
                after(eng, "m_l2", g.before(1), NCH, NCH + s - 1)

        NCONST = 19
        xg = x.rearrange("(n g) t f -> n t g f", g=G)
        og = out.rearrange("(n g) t f -> n t g f", g=G)
        block = ctx.enter_context(nc.Block())

        @block.sync
        def _(sp):
            def const(dst, src):
                sp.dma_start(dst, src).then_inc(sem("const_in"), 16)

            const(adj_i[:, :], adj)
            const(Wg[0][:, 0:P], W_0)
            const(Wg[1][:, 0:P], W_1)
            for l, a in enumerate((a_0, a_1)):
                const(arow[:, l, :, :], a.rearrange("(o k f) u -> o k (f u)", o=1, k=2).broadcast_to([P, 2, P]))
            const(gcol[:, :], gamma.rearrange("(p u) -> p u", u=1))
            const(bcol[:, :], beta.rearrange("(p u) -> p u", u=1))
            const(b1row[:, :], b1_0.rearrange("e (c p) -> (e c) p", c=C0))
            const(wr_sb[:, :], Wr)
            const(brow[:, :], br.rearrange("(u e) -> u e", u=1).broadcast_to([P, E0]))
            const(rw_row[:, :], rw)
            const(rbrow[:, :], rb.rearrange("(u e) -> u e", u=1).broadcast_to([P, E1]))
            const(w1raw[:, :].rearrange("p (e h) -> p e h", e=E0), W1_0.rearrange("e d h -> d e h"))
            const(w2raw[:, :, :], W2_0.rearrange("e (c p) d -> p (e c) d", c=C0))
            const(v1raw[:, :].rearrange("p (e h) -> p e h", e=E1), W1_1.rearrange("e d h -> d e h"))
            const(v2raw[:, :, :], W2_1.rearrange("(c q) h d -> (q h) c d", c=NCH))
            for r in range(2):
                const(c2raw[32 * r:32 * r + 32, :], b2_1)
            const(b2row[:, :], b2_0)
            for r in range(2):
                sp.dma_start(selraw[32 * r:32 * r + 32, :].rearrange("e (f h) -> e f h", f=E1),
                             b1_1.rearrange("e (u h) -> e u h", u=1).broadcast_to([E1, E1, H1])).then_inc(sem("b1_in"), 16)

            def load(g):
                if g.before(2).live():
                    sp.wait_ge(sem(f"kept{g.par}"), 16 * g.half)
                sp.dma_start(x0[g.par][:, :, :], xg[g.n]).then_inc(sem(f"x0_in{g.par}"), 16)

            @each
            def body(j, p):
                g = At(j, p, LAG["A"])
                if g.live():
                    load(g)
                g = At(j, p, LAG["a"])
                if g.live():
                    if g.before(2).live():
                        after(sp, "x1", g.before(2))
                    else:
                        after(sp, "xnA", g)
                    sp.dma_start(x0k[g.par][:, :, :], x0[g.par][:, :, :]).then_inc(sem(f"kept{g.par}"), 16)
                g = At(j, p, LAG["O"])
                if g.live():
                    after(sp, "fin", g)
                    sp.dma_start(og[g.n], fin[g.par][:, :, :]).then_inc(sem(f"stored{g.par}"), 16)

            body(sp)
            for p in range(2):
                sp.wait_ge(sem(f"stored{p}"), 16 * (NGROUP // 2))

        @block.gpsimd
        def _(pool):
            pool.memset(neghalf[:, :], -0.5)
            pool.memset(eps[:, :], EPS)
            pool.memset(ident[:, :], 0.0).then_inc(sem("zeroed"), 1)
            pool.wait_ge(sem("zeroed"), 1)
            pool.affine_select(out=ident[:, :], in_=ident[:, :], compare_op=ALU.not_equal, fill=1.0, base=0,
                               pattern=[[-1, P]], channel_multiplier=1).then_inc(sem("ident"), 1)
            for r in range(2):
                pool.wait_ge(sem("spread_raw"), r + 1)
                part = spread_f[:, :].rearrange("r (e p) -> r e p", e=E0)
                pool.affine_select(out=part, in_=part, compare_op=ALU.not_equal, fill=1.0, base=-(WHI, WLO)[r],
                                   pattern=[[-1, E0], [0, P]], channel_multiplier=1).then_inc(sem("spread_raw"), 1)
            pool.wait_ge(sem("spread_raw"), 3)
            pool.iota(iota_i[:, :], pattern=[[1, E1]], base=0, channel_multiplier=0).then_inc(sem("iota"), 1)
            pool.wait_ge(sem("b1_in"), 32)
            pool.wait_ge(sem("masked"), 1)
            pool.wait_ge(sem("iota"), 1)
            for r in range(3):
                if r:
                    pool.wait_ge(sem("sel_raw"), r)
                part = selraw[32 * r:32 * r + 32, :].rearrange("e (f h) -> e f h", f=E1)
                pool.affine_select(out=part, in_=part, compare_op=ALU.is_equal, fill=0.0, base=0,
                                   pattern=[[-1, E1], [0, H1]], channel_multiplier=1).then_inc(sem("sel_raw"), 1)

            def rstd(k, g):
                after(pool, f"moments{k}", g)
                pool.tensor_tensor(ve[k][:, :], mv[k][:, :, 1], eps[:, :], ALU.add).then_inc(sem(f"var_eps{k}"), 1)
                after(pool, f"var_eps{k}", g)
                if k != "C":
                    after(pool, f"xn{k}", g.before(1))
                    pool.tensor_tensor(rs[k][:, :], ve[k][:, :], neghalf[:, :], ALU.pow).then_inc(sem(f"rstd{k}"), 1)
                    return
                c = [v2t[:, n, :] for n in range(4)]
                pool.tensor_tensor(c[0], ve[k][:, :], neghalf[:, :], ALU.pow).then_inc(sem("second"), 1)
                after(pool, "second", g, 5, 1)
                pool.tensor_tensor(c[1], c[0], c[0], ALU.mult).then_inc(sem("second"), 1)
                after(pool, "second", g, 5, 2)
                pool.tensor_tensor(c[2], c[1], mv[k][:, :, 1], ALU.mult).then_inc(sem("second"), 1)
                after(pool, "second", g, 5, 3)
                pool.tensor_tensor(c[1], c[2], eps[:, :], ALU.add).then_inc(sem("second"), 1)
                after(pool, "second", g, 5, 4)
                pool.tensor_tensor(c[3], c[1], neghalf[:, :], ALU.pow).then_inc(sem("second"), 1)
                after(pool, "second", g, 5, 5)
                after(pool, f"xn{k}", g.before(1))
                pool.tensor_tensor(rs[k][:, :], c[0], c[3], ALU.mult).then_inc(sem(f"rstd{k}"), 1)

            @each
            def body(j, p):
                at = stages(j, p)
                for s in range(SLOTS):
                    g = at["D"]
                    if g.live():
                        after(pool, "hhi1", g, E0, s + 1)
                        l2_done(pool, g, s)
                        pool.tensor_tensor(hlo[s % 2][1][:, :], hid[s % 2][1][:, :], hhi[s % 2][1][:, :].bitcast(F32),
                                           ALU.subtract).then_inc(sem("hlo1"), 1)
                    for k, slot in (("C", 2), ("F", 4), ("E", 5)):
                        if s == slot and at[k].live():
                            rstd(k, at[k])
                    g, e = (at["D"].before(1), SLOTS - 1) if s == 0 else (at["D"], s - 1)
                    if g.live() and e >= 1:
                        after(pool, "ym", g, SLOTS, e + 1)
                        if e >= 2:
                            after(pool, "ysum", g, SLOTS - 1, e - 1)
                        to = acc[g.par]
                        pool.tensor_tensor(to[:, :], to[:, :], ym[e % 2][:, :], ALU.add).then_inc(sem("ysum"), 1)
                    if s == 0 and at["A"].live():
                        rstd("A", at["A"])

            body(pool)

        @block.scalar
        def _(act):
            def xT_out(k, g):
                after(act, f"xn_ps{k}", g)
                if k in "AE":
                    after(act, f"s_ps{k}", g.before(1))
                    act.activation(xnT[k][:, :], TPB[k][:, :], ACT.Copy).then_inc(sem(f"xnT{k}"), 1)
                    return
                after(act, f"lg_ps{k}", g.before(1))
                after(act, f"xlo{k}", g.before(1))
                user, n = ("d_l1", E0 * C0) if k == "C" else ("m_l1", NCH)
                if k == "C":
                    act.activation(xnT[k][:, :], TPB[k][:, :], ACT.Identity, scale=gcol[:, 0:1], bias=bcol[:, 0:1])
                    after(act, user, g.before(2), n, n)
                    act.activation(xhi[k][g.par][:, :], TPB[k][:, :], ACT.Identity, scale=gcol[:, 0:1],
                                   bias=bcol[:, 0:1]).then_inc(sem(f"xnT{k}"), 1)
                else:
                    act.activation(xnT[k][:, :], TPB[k][:, :], ACT.Copy)
                    after(act, user, g.before(2), n, n)
                    act.activation(xhi[k][g.par][:, :], TPB[k][:, :], ACT.Copy).then_inc(sem(f"xnT{k}"), 1)

            def h_out(k, g):
                after(act, f"h_ps{k}", g)
                after(act, f"att_ps{'B' if k == 'A' else 'F'}", g.before(2))
                act.activation(hg[k][g.par][:, 0:G - 1, :], h3(k)[:, :, 0:P], ACT.Copy)
                act.activation(hg[k][g.par][:, G - 1, :], h4(k)[:, 0:P], ACT.Copy).then_inc(sem(f"h{k}"), 1)

            def prT_out(k, g):
                after(act, f"pr_ps{k}", g)
                after(act, f"att_ps{k}", g.before(1))
                act.activation(prT[k][:, :], TP1[:, :], ACT.Copy).then_inc(sem(f"prT{k}"), 1)

            def exps(at):
                for k, src in (("F", "E"), ("B", "A")):
                    g = at[k]
                    if g.live():
                        after(act, f"score{src}", g)
                        after(act, f"pr_ps{k}", g.before(1))
                        after(act, f"rsum{k}", g.before(1))
                        act.activation(pr[k][:, :, :], sc[src][:, :, :], ACT.Exp).then_inc(sem(f"pr{k}"), 1)
                g = at["C"]
                if g.live():
                    after(act, "zneg", g)
                    act.activation(zneg[:, :, :], zneg[:, :, :], ACT.Exp).then_inc(sem("eneg"), 1)

            @each
            def body(j, p):
                at = stages(j, p)
                for s in range(SLOTS):
                    g = at["D"]
                    if g.live():
                        for c in range(C0):
                            n = C0 * s + c
                            after(act, "d_l1", g, E0 * C0, n + 1)
                            if s >= 2:
                                after(act, f"hlo{c}", g, E0, s - 1)
                            else:
                                after(act, f"hlo{c}", g.before(1), E0, E0 + s - 1)
                            act.activation(hid[s % 2][c][:, :], ZB[c][:, :], ACT.Gelu,
                                           bias=b1col[:, n:n + 1]).then_inc(sem("gelu"), 1)
                        for c in range(C0):
                            after(act, "gelu", g, E0 * C0, C0 * s + c + 1)
                            l2_done(act, g, s)
                            act.activation(hhi[s % 2][c][:, :], hid[s % 2][c][:, :], ACT.Copy).then_inc(sem(f"hhi{c}"), 1)
                    g = at["M"]
                    if g.live():
                        after(act, "m_l1", g, NCH, s + 1)
                        m2_done(act, g, s)
                        act.activation(rhi[s % 2][:, :], ZB[0][:, :], ACT.Relu).then_inc(sem("relu"), 1)
                    g = at["D"]
                    if g.live():
                        after(act, "wb_ps", g, E0, s + 1)
                        if s >= 2:
                            after(act, "ym", g, E0, s - 1)
                        else:
                            after(act, "ym", g.before(1), E0, E0 + s - 1)
                        act.activation(wb[s % 2][:, :], ZB[1][:, :], ACT.Copy).then_inc(sem("wb"), 1)
                    g = at["M"].before(1)
                    if s == 0 and g.live():
                        after(act, "m_l2", g, NCH, NCH)
                        after(act, "out_ps", g.before(1))
                        act.activation(oT[:, :], OB[:, :], ACT.Relu).then_inc(sem("oT"), 1)
                    if s == 0:
                        exps(at)
                    if s == 1:
                        for k in "ae":
                            after(act, f"s1{k.upper()}", at[k])
                        for k in "ae":
                            if at[k].live():
                                h_out(k.upper(), at[k])
                    if s == 2 and at["A"].live():
                        xT_out("A", at["A"])
                    if s == 2 and at["F"].live():
                        prT_out("F", at["F"])
                    if s == 4:
                        if at["C"].live():
                            xT_out("C", at["C"])
                        if at["B"].live():
                            prT_out("B", at["B"])
                    if s == 5 and at["F"].live():
                        xT_out("F", at["F"])
                    if s == 6 and at["C"].live():
                        after(act, "dif", at["C"])
                        act.activation(th[:, :], dif[:, :], ACT.Tanh, scale=0.5).then_inc(sem("tanh"), 1)
                    if s == 7:
                        if at["E"].live():
                            xT_out("E", at["E"])
                        g = at["W"]
                        if g.live():
                            after(act, "wo_ps", g)
                            after(act, "wb_ps", at["C"].before(2), E0, E0)
                            after(act, "m_l1", at["F"].before(2), NCH, NCH)
                            after(act, "m_l2", at["F"].before(2), NCH, NCH)
                            act.activation(woT[g.par][:, :], TP0[:, :], ACT.Copy).then_inc(sem("woT"), 1)

            body(act)

        @block.vector
        def _(dve):
            steps = [0]

            def link(ins):
                steps[0] += 1
                ins.then_inc(sem("setup_v"), 1)
                dve.wait_ge(sem("setup_v"), steps[0])

            dve.memset(selraw[96:P, :], 0.0)
            dve.memset(selraw[64:96, :], MASKED).then_inc(sem("masked"), 1)
            dve.memset(ones[:, :], 1.0)
            dve.memset(wo[:, :, :], 0.0)
            dve.memset(spread_f[:, :], 0.0).then_inc(sem("spread_raw"), 1)
            dve.wait_ge(sem("const_in"), 16 * NCONST)
            dve.tensor_copy(adj_f[:, :], adj_i[:, :])
            dve.tensor_copy(w1hi[:, :], w1raw[:, :])
            dve.tensor_copy(v1hi[:, :], v1raw[:, :])
            dve.tensor_copy(w2hi[:, :, :], w2raw[:, :, :])
            dve.tensor_copy(v2hi[:, :, :], v2raw[:, :, :])
            dve.tensor_copy(c2hi[:, :], c2raw[:, :])
            link(dve.tensor_tensor(wprod[:, 0, :, :], Wg[0][:, 0:P].unsqueeze(1).broadcast_to([P, 2, P]), arow[:, 0, :, :], ALU.mult))
            link(dve.tensor_tensor(wprod[:, 1, :, :], Wg[1][:, 0:P].unsqueeze(1).broadcast_to([P, 2, P]), arow[:, 1, :, :], ALU.mult))
            dve.tensor_tensor(w1lo[:, :], w1raw[:, :], w1hi[:, :].bitcast(F32), ALU.subtract)
            dve.tensor_tensor(v1lo[:, :], v1raw[:, :], v1hi[:, :].bitcast(F32), ALU.subtract)
            dve.tensor_tensor(w2lo[:, :, :], w2raw[:, :, :], w2hi[:, :, :].bitcast(F32), ALU.subtract)
            dve.tensor_tensor(v2lo[:, :, :], v2raw[:, :, :], v2hi[:, :, :].bitcast(F32), ALU.subtract)
            dve.tensor_copy(c2[0:32, :], c2hi[0:32, :].bitcast(F32))
            dve.tensor_tensor(c2[32:64, :], c2raw[32:64, :], c2hi[32:64, :].bitcast(F32), ALU.subtract)
            dve.tensor_scalar(adj_m[:, 0, :], adj_f[:, :], 0.0, 1.0, ALU.is_gt, ALU.subtract)
            link(dve.tensor_scalar(adj_m[:, 1, :], adj_f[:, :], 0.0, 1.0, ALU.not_equal, ALU.subtract))
            for l in range(2):
                dve.tensor_scalar(mask[l][:, :], adj_m[:, l, :], -MASKED, None, ALU.mult)
            link(dve.reduce_sum(wa[:, :, :], wprod[:, :, :, :], AX.X))
            for l in range(2):
                dve.tensor_copy(Wg[l][:, P:P + 1], wa[:, l, 0:1])
                dve.tensor_scalar(wa2rep[l][:, :], ones[:, :], wa[:, l, 1:2], None, ALU.mult)
            dve.wait_ge(sem("ident"), 1)
            dve.tensor_copy(identb[:, :], ident[:, :])
            dve.wait_ge(sem("iota"), 1)
            dve.tensor_copy(iota[:, :], iota_i[:, :])
            dve.wait_ge(sem("spread_raw"), 3)
            dve.tensor_copy(spread[:, :], spread_f[:, :])
            dve.wait_ge(sem("sel_raw"), 3)
            link(dve.tensor_copy(selhi[:, :], selraw[:, :]))
            dve.tensor_copy(sel[0:32, :], selhi[0:32, :].bitcast(F32))
            dve.tensor_tensor(sel[32:64, :], selraw[32:64, :], selhi[32:64, :].bitcast(F32), ALU.subtract)
            dve.tensor_copy(sel[64:P, :], selhi[64:P, :].bitcast(F32)).then_inc(sem("consts"), 1)
            dve.wait_ge(sem("cols_ps"), 1)
            dve.tensor_copy(rwT[:, :], TP0[:, 0:E1])
            dve.tensor_copy(b2col[:, :], TP0[:, E1 + E0 * C0:E1 + E0 * C0 + E0])
            dve.tensor_copy(b1col[:, :], TP0[:, E1:E1 + E0 * C0]).then_inc(sem("cols"), 1)
            dve.wait_ge(sem("cols"), 1)

            def stats(k, g, xin):
                for n in range(G):
                    last = dve.bn_stats(st[k][:, n, :], xin[:, n, :])
                last.then_inc(sem(f"stats{k}"), 1)
                after(dve, f"stats{k}", g)
                after(dve, f"rstd{k}", g.before(1))
                settle()
                for n in range(G):
                    last = dve.bn_aggr(mv[k][:, n, :], st[k][:, n, :])
                last.then_inc(sem(f"moments{k}"), 1)

            def norm(k, g, xin):
                after(dve, f"rstd{k}", g)
                after(dve, f"xn_ps{k}", g.before(1))
                for n in range(G):
                    last = dve.tensor_scalar(xn[k][:, n, :], xin[:, n, :], mv[k][:, n, 0:1], rs[k][:, n:n + 1],
                                             ALU.subtract, ALU.mult)
                last.then_inc(sem(f"xn{k}"), 1)

            def s1_out(k, g):
                after(dve, f"h_ps{k}", g)
                after(dve, f"raw{k}", g.before(1))
                dve.tensor_copy(s1[k][:, 0:G - 1], h3(k)[:, :, P])
                dve.tensor_copy(s1[k][:, G - 1:G], h4(k)[:, P:P + 1]).then_inc(sem(f"s1{k}"), 1)

            def raw_scores(k, g):
                after(dve, f"s1{k}", g)
                after(dve, f"s_ps{k}", g)
                after(dve, f"leaky{k}", g.before(1))
                dve.tensor_tensor(tt[k][:, :, :], g4(SB), s1[k][:, :].unsqueeze(2).broadcast_to([P, G, P]),
                                  ALU.add).then_inc(sem(f"raw{k}"), 1)

            def scores(k, g):
                l = "AE".index(k)
                after(dve, f"raw{k}", g)
                after(dve, f"pr{'B' if k == 'A' else 'F'}", g.before(1))
                dve.scalar_tensor_tensor(sc[k][:, :, :], tt[k][:, :, :], SLOPE[l], tt[k][:, :, :], ALU.mult,
                                         ALU.max).then_inc(sem(f"leaky{k}"), 1)
                after(dve, f"leaky{k}", g)
                dve.reduce_max(em[k][:, :], sc[k][:, :, :], AX.X).then_inc(sem(f"rowmax{k}"), 1)
                after(dve, f"rowmax{k}", g)
                dve.tensor_tensor(sc[k][:, :, :], sc[k][:, :, :], em[k][:, :].unsqueeze(2).broadcast_to([P, G, P]),
                                  ALU.subtract).then_inc(sem(f"score{k}"), 1)

            def row_sums(k, g):
                after(dve, f"pr{k}", g)
                dve.reduce_sum(rsum[k][:, :], pr[k][:, :, :], AX.X).then_inc(sem(f"rsum{k}"), 1)
                after(dve, f"rsum{k}", g)
                after(dve, f"z{k}", g.before(1))
                dve.reciprocal(rinv[k][:, :], rsum[k][:, :]).then_inc(sem(f"rinv{k}"), 1)

            def attended(k, g):
                after(dve, f"rinv{k}", g)
                after(dve, f"att_ps{k}", g)
                if k == "B":
                    after(dve, "x1a", g.before(1))
                dve.tensor_tensor(z[k][:, :, :], g4(HB), rinv[k][:, :].unsqueeze(2).broadcast_to([P, G, P]),
                                  ALU.mult).then_inc(sem(f"z{k}"), 1)
                after(dve, f"z{k}", g)

            def logits(k, g, bias, n):
                after(dve, f"lg_ps{k}", g)
                dve.tensor_tensor(lg[k][:, :, :], SB[:, 0:G * n].rearrange("p (g e) -> p g e", g=G),
                                  bias[:, :].unsqueeze(1).broadcast_to([P, G, n]), ALU.add).then_inc(sem(f"lg{k}"), 1)
                after(dve, f"lg{k}", g)
                settle()
                for q in range(G):
                    last = dve.max(top[k][:, q, :], lg[k][:, q, :])
                last.then_inc(sem(f"top{k}"), 1)
                after(dve, f"top{k}", g)
                settle()
                for q in range(G):
                    last = dve.max_index(idx[k][:, q, :], top[k][:, q, :], lg[k][:, q, :])
                last.then_inc(sem(f"idx{k}"), 1)
                after(dve, f"idx{k}", g)
                dve.tensor_copy(idf[k][:, :, :], idx[k][:, :, 0:2]).then_inc(sem(f"idf{k}"), 1)

            @each
            def body(j, p):
                at = stages(j, p)
                A, B, C, D, E, F, M, O, W = (at[k] for k in "ABCDEFMOW")
                for s in range(SLOTS):
                    if s == 5 and F.live():
                        after(dve, "xn_psE", E.before(1))
                        norm("F", F, x3[F.par])
                    if s == 7 and E.live():
                        after(dve, "xn_psF", F)
                        norm("E", E, x2[E.par])
                    if D.live():
                        after(dve, "hhi0", D, E0, s + 1)
                        l2_done(dve, D, s)
                        dve.tensor_tensor(hlo[s % 2][0][:, :], hid[s % 2][0][:, :], hhi[s % 2][0][:, :].bitcast(F32),
                                          ALU.subtract).then_inc(sem("hlo0"), 1)
                    if s == 1:
                        after(dve, "h_psE", at["e"])
                        for k in "ae":
                            if at[k].live():
                                s1_out(k.upper(), at[k])
                        if at["a"].live():
                            raw_scores("A", at["a"])
                    if M.live():
                        after(dve, "relu", M, NCH, s + 1)
                        m2_done(dve, M, s)
                        dve.scalar_tensor_tensor(rlo[s % 2][:, :], ZB[0][:, :], 0.0,
                                                 rhi[s % 2][:, :].bitcast(F32), ALU.max,
                                                 ALU.subtract).then_inc(sem("rlo"), 1)
                    g, e = (D.before(1), SLOTS - 1) if s == 0 else (D, s - 1)
                    if g.live():
                        after(dve, "d_l2", g, E0, e + 1)
                        after(dve, "wb", g, E0, e + 1)
                        if e == 0:
                            after(dve, "y_ps", g.before(2))
                            to = acc[g.par]
                        else:
                            to = ym[e % 2]
                            if e >= 3:
                                after(dve, "ysum", g, SLOTS - 1, e - 2)
                            else:
                                after(dve, "ysum", g.before(1), SLOTS - 1, SLOTS - 1 + min(e - 2, 0))
                        dve.scalar_tensor_tensor(to[:, :], YB[:, :], b2col[:, e:e + 1], wb[e % 2][:, :], ALU.add,
                                                 ALU.mult).then_inc(sem("ym"), 1)
                    if s == 0 and A.live():
                        dve.wait_ge(sem(f"x0_in{A.par}"), 16 * (A.half + 1))
                        stats("A", A, x0[A.par])
                        after(dve, "xn_psC", C.before(1))
                        norm("A", A, x0[A.par])
                    if s == 1:
                        if at["e"].live():
                            raw_scores("E", at["e"])
                        if C.live():
                            after(dve, "x1c", C.before(1))
                            dve.wait_ge(sem(f"kept{C.par}"), 16 * (C.half + 1))
                            dve.scalar_tensor_tensor(x1n[:, :, :], z["B"][:, :, :], 0.0, x0k[C.par][:, :, :], ALU.max,
                                                     ALU.add).then_inc(sem("x1a"), 1)
                            after(dve, "x1a", C)
                            after(dve, "eneg", C)
                            dve.scalar_tensor_tensor(x1n[:, :, :], zneg[:, :, :], 1.0, x1n[:, :, :],
                                                     ALU.subtract, ALU.add).then_inc(sem("x1"), 1)
                            after(dve, "x1", C)
                            stats("C", C, x1n)
                    if s == 2:
                        if F.live():
                            row_sums("F", F)
                        if B.live():
                            row_sums("B", B)
                        if O.live():
                            after(dve, "out_ps", O)
                            if O.before(2).live():
                                dve.wait_ge(sem(f"stored{O.par}"), 16 * O.half)
                            dve.tensor_tensor(fin[O.par][:, :, :], g4(TP0), x3[O.par][:, :, :], ALU.add).then_inc(sem("fin"), 1)
                    if s == 3:
                        if F.live():
                            attended("F", F)
                            after(dve, "fin", F.before(2))
                            dve.scalar_tensor_tensor(x3[F.par][:, :, :], z["F"][:, :, :], 0.0, x2[F.par][:, :, :], ALU.max,
                                                     ALU.add).then_inc(sem("x3"), 1)
                            after(dve, "x3", F)
                            stats("F", F, x3[F.par])
                        if C.live():
                            after(dve, "xn_psA", A)
                            norm("C", C, x1n)
                        if E.live():
                            after(dve, "y_ps", E)
                            after(dve, "x3", E.before(2))
                            dve.tensor_tensor(x2[E.par][:, :, :], g4(TP0), x1[E.par][:, :, :], ALU.add).then_inc(sem("x2"), 1)
                    if s == 4:
                        if E.live():
                            after(dve, "x2", E)
                            stats("E", E, x2[E.par])
                        if at["a"].live():
                            scores("A", at["a"])
                        if C.live():
                            after(dve, "x2", C.before(2))
                            dve.tensor_copy(x1[C.par][:, :, :], x1n[:, :, :]).then_inc(sem("x1c"), 1)
                    if s == 5:
                        if C.live():
                            after(dve, "xnTC", C)
                            after(dve, "d_l1", C.before(2), E0 * C0, E0 * C0)
                            dve.tensor_tensor(xlo["C"][C.par][:, :], xnT["C"][:, :], xhi["C"][C.par][:, :].bitcast(F32),
                                              ALU.subtract).then_inc(sem("xloC"), 1)
                            logits("C", C, brow, E0)
                            after(dve, "tanh", C.before(1))
                            dve.tensor_tensor(dif[:, :], top["C"][:, :, 0], top["C"][:, :, 1], ALU.subtract).then_inc(sem("dif"), 1)
                            after(dve, "idfC", C)
                            for n in range(2):
                                dve.tensor_tensor(oh2[:, n, :, :], iota[:, 0:E0].unsqueeze(1).broadcast_to([P, G, E0]),
                                                  idf["C"][:, :, n:n + 1].broadcast_to([P, G, E0]),
                                                  ALU.is_equal).then_inc(sem("oh2"), 1)
                    if s == 6:
                        if F.live():
                            after(dve, "xnTF", F)
                            after(dve, "m_l1", F.before(2), NCH, NCH)
                            dve.tensor_tensor(xlo["F"][F.par][:, :], xnT["F"][:, :], xhi["F"][F.par][:, :].bitcast(F32),
                                              ALU.subtract).then_inc(sem("xloF"), 1)
                            logits("F", F, rbrow, E1)
                            after(dve, "idfF", F)
                            after(dve, "wo_ps", W.before(1))
                            for r in range(3):
                                op = ALU.not_equal if r == 2 else ALU.is_equal
                                last = dve.tensor_tensor(wo[:, :, r * E1:(r + 1) * E1],
                                                         iota[:, :].unsqueeze(1).broadcast_to([P, G, E1]),
                                                         idf["F"][:, :, 0:1].broadcast_to([P, G, E1]), op)
                            last.then_inc(sem("ohc"), 1)
                        if C.live():
                            after(dve, "tanh", C)
                            dve.tensor_scalar(w01[:, 0, :], th[:, :], 0.5, 0.5, ALU.mult, ALU.add)
                            dve.tensor_scalar(w01[:, 1, :], th[:, :], -0.5, 0.5, ALU.mult, ALU.add).then_inc(sem("w01"), 1)
                            after(dve, "w01", C)
                            after(dve, "oh2", C, 2, 2)
                            dve.tensor_tensor(ohw[:, :, :, :], oh2[:, :, :, :],
                                              w01[:, :, :].unsqueeze(3).broadcast_to([P, 2, G, E0]),
                                              ALU.mult).then_inc(sem("ohw"), 1)
                            after(dve, "ohw", C)
                            dve.tensor_tensor(wgt[:, :, :], ohw[:, 0, :, :], ohw[:, 1, :, :], ALU.add).then_inc(sem("wgt"), 1)
                            after(dve, "wgt", C)
                            after(dve, "wo_ps", W.before(1))
                            dve.tensor_copy(wo[:, :, WHI:WHI + E0].bitcast(F32R), wgt[:, :, :]).then_inc(sem("whi"), 1)
                            after(dve, "whi", C)
                            dve.tensor_tensor(wo[:, :, WLO:WLO + E0], wgt[:, :, :], wo[:, :, WHI:WHI + E0],
                                              ALU.subtract).then_inc(sem("wcat"), 1)
                    if s == 7:
                        if B.live():
                            attended("B", B)
                            after(dve, "x1", B.before(1))
                            dve.tensor_scalar(zneg[:, :, :], z["B"][:, :, :], 0.0, None, ALU.min).then_inc(sem("zneg"), 1)
                        if at["e"].live():
                            scores("E", at["e"])

            body(dve)

        @block.tensor
        def _(pe):
            pe.wait_ge(sem("ident"), 1)
            pe.wait_ge(sem("const_in"), 16 * NCONST)
            pe.transpose(TP0[:, 0:E1], rw_row[:, :], ident[0:E1, 0:E1])
            pe.transpose(TP0[:, E1:E1 + E0 * C0], b1row[:, :], ident[0:E0 * C0, 0:E0 * C0])
            pe.transpose(TP0[:, E1 + E0 * C0:E1 + E0 * C0 + E0], b2row[:, :],
                         ident[0:E0, 0:E0]).then_inc(sem("cols_ps"), 1)
            pe.wait_ge(sem("consts"), 1)
            pe.wait_ge(sem("cols"), 1)

            def turn(bank, src, done, n=P):
                for q in range(G):
                    last = pe.transpose(bank[0:n, q * P:(q + 1) * P], src[:, q, :], ident[:, :])
                last.then_inc(sem(done), 1)

            def rows(k, g):
                after(pe, f"xn{k}", g)
                turn(TPB[k], xn[k], f"xn_ps{k}")

            def front_h(k, g):
                l = "AE".index(k)
                after(pe, f"xnT{k}", g)
                for q in range(G):
                    to = h3(k)[:, q, :] if q < G - 1 else h4(k)
                    last = pe.matmul(to, xnT[k][:, q * P:(q + 1) * P], Wg[l][:, :], start=(q in (0, G - 1)),
                                     stop=(q >= G - 2), skip_group_check=True)
                last.then_inc(sem(f"h_ps{k}"), 1)

            def front_s(k, g):
                l = "AE".index(k)
                pe.matmul(SB[:, :], wa2rep[l][:, :], xnT[k][:, :], start=True, stop=False)
                pe.matmul(g4(SB), identb[:, :], mask[l][:, :].unsqueeze(1).broadcast_to([P, G, P]), start=False,
                          stop=True).then_inc(sem(f"s_ps{k}"), 1)

            def attend(k, src, g):
                after(pe, f"prT{k}", g)
                for q in range(G):
                    last = pe.matmul(HB[:, q * P:(q + 1) * P], prT[k][:, q * P:(q + 1) * P], hg[src][g.par][:, q, 0:P],
                                     start=(q == 0), stop=(q == G - 1), skip_group_check=True)
                last.then_inc(sem(f"att_ps{k}"), 1)

            def route(k, g, w, n):
                after(pe, f"xnT{k}", g)
                for q in range(G):
                    last = pe.matmul(SB[:, q * n:(q + 1) * n], xnT[k][:, q * P:(q + 1) * P], w[:, :],
                                     start=(q == 0), stop=(q == G - 1), skip_group_check=True)
                last.then_inc(sem(f"lg_ps{k}"), 1)

            @each
            def body(j, p):
                at = stages(j, p)
                A, B, C, D, E, F, M, O, W = (at[k] for k in "ABCDEFMOW")

                def split(out_, w_hi, w_lo, k, g, stop, done):
                    hi, lo = xhi[k][g.par], xlo[k][g.par]
                    pe.matmul(out_[:, :], w_hi, hi[:, :], start=True, stop=False)
                    pe.matmul(out_[:, :], w_lo, hi[:, :], start=False, stop=False)
                    last = pe.matmul(out_[:, :], w_hi, lo[:, :], start=False, stop=stop)
                    if stop:
                        last.then_inc(sem(done), 1)

                def z_free(bank, s, first):
                    if first and bank == 0:
                        after(pe, "gelu", D, E0 * C0, C0 * s)
                        after(pe, "rlo", M, NCH, s)
                    elif first:
                        after(pe, "wb", D, E0, s)
                    elif bank == 0:
                        after(pe, "gelu", D, E0 * C0, C0 * s + 1)
                        after(pe, "rlo", M, NCH, s)
                    else:
                        after(pe, "gelu", D, E0 * C0, C0 * (s + 1))

                def first_layer(s, c):
                    n = C0 * s + c
                    z_free(c, s, True)
                    w = slice(n * P, (n + 1) * P)
                    split(ZB[c], w1hi[:, w], w1lo[:, w], "C", D, True, "d_l1")

                def second_layer(g, e):
                    if e == 0:
                        after(pe, "ym", g.before(1), E0, E0)
                    else:
                        after(pe, "ym", g, E0, e)
                    for c in range(C0):
                        after(pe, f"hhi{c}", g, E0, e + 1)
                        hi, n = hhi[e % 2][c], C0 * e + c
                        pe.matmul(YB[:, :], w2hi[:, n, :], hi[:, :], start=(c == 0), stop=False)
                        pe.matmul(YB[:, :], w2lo[:, n, :], hi[:, :], start=False, stop=False)
                    for c in range(C0):
                        after(pe, f"hlo{c}", g, E0, e + 1)
                        last = pe.matmul(YB[:, :], w2hi[:, C0 * e + c, :], hlo[e % 2][c][:, :], start=False,
                                         stop=(c == C0 - 1))
                    last.then_inc(sem("d_l2"), 1)

                users = {
                    "TP0": (("hA", at["a"]), ("hE", at["e"]), ("xnTA", A), ("fin", O), ("x2", E), ("xnTC", C), ("woT", W)),
                    "TP1": (("hE", at["e"]), ("prTF", F), ("prTB", B), ("xnTF", F), ("xnTE", E)),
                    "H": (("hA", at["a"]), ("zF", F), ("zB", B)),
                    "S": (("rawA", at["a"]), ("rawE", at["e"]), ("lgC", C), ("lgF", F)),
                }

                def free(bank, n):
                    for m, (name, g) in enumerate(users[bank]):
                        after(pe, name, g if m < n else g.before(1))

                def second_chunk(g, c):
                    if c == 0:
                        after(pe, "oT", g.before(1))
                    after(pe, "rlo", g, NCH, c + 1)
                    pe.matmul(OB[:, :], v2hi[:, c, :], rhi[c % 2][:, :], start=(c == 0), stop=False)
                    pe.matmul(OB[:, :], v2lo[:, c, :], rhi[c % 2][:, :], start=False, stop=False)
                    last = pe.matmul(OB[:, :], v2hi[:, c, :], rlo[c % 2][:, :], start=False, stop=False)
                    if c == NCH - 1:
                        last = pe.matmul(OB[:, :], c2[:, :], woT[g.par][0:2 * E1, :], start=False, stop=True)
                    last.then_inc(sem("m_l2"), 1)

                for s in range(SLOTS):
                    if D.live():
                        if s == 0:
                            after(pe, "xloC", D)
                        first_layer(s, 0)
                        first_layer(s, 1)
                    g, c = (M.before(1), NCH - 1) if s == 0 else (M, s - 1)
                    if g.live():
                        second_chunk(g, c)
                    if s == 1:
                        a, b = at["a"], at["e"]
                        if a.live():
                            free("H", 0)
                            free("TP0", 0)
                            front_h("A", a)
                        if b.live():
                            free("TP1", 0)
                            for m, (name, g) in enumerate(users["TP0"]):
                                if m != 0:
                                    after(pe, name, g.before(1))
                            front_h("E", b)
                        if a.live():
                            free("S", 0)
                            front_s("A", a)
                    if M.live():
                        if s == 0:
                            after(pe, "xloF", M)
                            after(pe, "woT", W.before(1))
                        z_free(0, s, False)
                        w = slice(s * P, (s + 1) * P)
                        zb = ZB[0]
                        split(zb, v1hi[:, w], v1lo[:, w], "F", M, False, None)
                        pe.matmul(zb[:, :], sel[:, w], woT[M.par][:, :], start=False, stop=True).then_inc(sem("m_l1"), 1)
                    if D.live():
                        if s == 0:
                            after(pe, "woT", W.before(1))
                        z_free(1, s, False)
                        pe.matmul(ZB[1][:, :], spread[:, s * P:(s + 1) * P], woT[D.par][:, :], start=True,
                                  stop=True).then_inc(sem("wb_ps"), 1)
                    g, e = (D.before(1), SLOTS - 1) if s == 0 else (D, s - 1)
                    if g.live():
                        second_layer(g, e)
                    if s == 1 and at["e"].live():
                        free("S", 1)
                        front_s("E", at["e"])
                    if s == 1 and A.live():
                        free("TP0", 2)
                        rows("A", A)
                    if s == 2:
                        if F.live():
                            free("TP1", 1)
                            after(pe, "prF", F)
                            turn(TP1, pr["F"], "pr_psF")
                        if O.live():
                            after(pe, "oT", O)
                            free("TP0", 3)
                            for q in range(G):
                                last = pe.transpose(TP0[:, q * P:(q + 1) * P], oT[:, q * P:(q + 1) * P], ident[:, :])
                            last.then_inc(sem("out_ps"), 1)
                    if s == 3:
                        if F.live():
                            free("H", 1)
                            attend("F", "E", F)
                        if E.live():
                            free("TP0", 4)
                            after(pe, "ysum", E, SLOTS - 1, SLOTS - 1)
                            for q in range(G):
                                last = pe.transpose(TP0[:, q * P:(q + 1) * P], acc[E.par][:, q * P:(q + 1) * P], ident[:, :])
                            last.then_inc(sem("y_ps"), 1)
                    if s == 4:
                        if C.live():
                            free("TP0", 5)
                            rows("C", C)
                        if B.live():
                            free("TP1", 2)
                            after(pe, "prB", B)
                            turn(TP1, pr["B"], "pr_psB")
                    if s == 5:
                        if F.live():
                            free("TP1", 3)
                            rows("F", F)
                        if C.live():
                            free("S", 2)
                            route("C", C, wr_sb, E0)
                    if s == 6:
                        if F.live():
                            free("S", 3)
                            route("F", F, rwT, E1)
                        if B.live():
                            free("H", 2)
                            attend("B", "A", B)
                    if s == 7:
                        if E.live():
                            free("TP1", 4)
                            rows("E", E)
                        if W.live():
                            free("TP0", 6)
                            after(pe, "wcat", C)
                            after(pe, "ohc", F)
                            turn(TP0, wo, "wo_ps")

            body(pe)


_INS = ["x", "adj", "L0_gnn_W", "L0_gnn_a", "L0_ffn_gamma", "L0_ffn_beta", "L0_ffn_Wr", "L0_ffn_br", "L0_ffn_W1",
        "L0_ffn_b1", "L0_ffn_W2", "L0_ffn_b2", "L1_gnn_W", "L1_gnn_a", "L1_ffn_router_w", "L1_ffn_router_b",
        "L1_ffn_W1", "L1_ffn_b1", "L1_ffn_W2", "L1_ffn_b2"]


def kernel(**inputs):
    import numpy as np
    import concourse.bacc as bacc
    from concourse.bass_utils import run_bass_kernel_spmd

    nc = bacc.Bacc("TRN2", target_bir_lowering=False, num_devices=1)
    arrays, args = {}, []
    for name in _INS:
        a = np.ascontiguousarray(inputs[name])
        arrays[f"in_{name}"] = a
        args.append(nc.dram_tensor(f"in_{name}", a.shape, mybir.dt.from_np(a.dtype), kind="ExternalInput").ap())
    o = nc.dram_tensor("out", [NGRAPH, P, P], F32, kind="ExternalOutput").ap()
    program(nc, *args, o)
    r = run_bass_kernel_spmd(nc, [arrays], core_ids=[0])
    return r.results[0]["out"]
```

```python
from contextlib import ExitStack

import concourse.bass as bass
from concourse import mybir

F32 = mybir.dt.float32
F32R = mybir.dt.float32r
BF16 = mybir.dt.bfloat16
I32 = mybir.dt.int32
U32 = mybir.dt.uint32
ALU = mybir.AluOpType
ACT = mybir.ActivationFunctionType
AX = mybir.AxisListType

P = 128
NGRAPH = 128
G = 4
T = G * P
NGROUP = NGRAPH // G
E0, H0 = 8, 256
C0 = H0 // P
E1, H1 = 32, 32
NCH = E1 * H1 // P
SLOTS = 8
assert E0 == SLOTS and NCH == SLOTS
EPS = 1e-5
SLOPE = (0.2, 0.01)
MASKED = -1e30

LAG = dict(A=0, a=1, B=2, C=3, D=4, E=5, e=6, F=7, M=8, O=9)
NITER = NGROUP + LAG["O"]
NTURN = NGROUP + LAG["F"] - LAG["C"]
FIRST = 12


class At:

    def __init__(self, j, p, lag, total=NGROUP):
        self.j, self.p, self.lag, self.total = j, p, lag, total
        self.n = 2 * j + (p - lag)
        self.fixed = isinstance(j, int)

    @property
    def par(self):
        return (self.p - self.lag) % 2

    @property
    def half(self):
        return self.j + (self.p - self.lag) // 2

    def live(self):
        return not self.fixed or 0 <= self.n < self.total

    def before(self, k):
        return At(self.j, self.p, self.lag + k, self.total)

    def count(self, per, k):
        if not self.fixed:
            return per * self.n + k
        if self.n < 0:
            return None
        return per * self.total if self.n >= self.total else per * self.n + k


def stages(j, p):
    at = {k: At(j, p, lag) for k, lag in LAG.items()}
    at["W"] = At(j, p, LAG["C"], NTURN)
    return at


def program(nc, x, adj, W_0, a_0, gamma, beta, Wr, br, W1_0, b1_0, W2_0, b2_0,
            W_1, a_1, rw, rb, W1_1, b1_1, W2_1, b2_1, out):
    ctx = ExitStack()
    with ctx:
        def sb(name, shape, dt=F32):
            return ctx.enter_context(nc.sbuf_tensor(name, shape, dt))

        def pb(name):
            return ctx.enter_context(nc.psum_tensor(name, [P, T], F32))

        sems = {}

        def sem(name):
            if name not in sems:
                sems[name] = ctx.enter_context(nc.semaphore(name))
            return sems[name]

        def after(eng, name, g, per=1, k=1):
            v = g.count(per, k)
            if v is not None:
                eng.wait_ge(sem(name), v)

        def settle():
            nc.vector.memset(spare[:, :], 0.0)

        WCOL = 3 * E1
        NWB = 4
        ident = sb("ident", [P, P])
        identb = sb("identb", [P, P], BF16)
        mask = [sb(f"mask{l}", [P, P], BF16) for l in range(2)]
        Wg = [sb(f"Wg{l}", [P, P + 1]) for l in range(2)]
        wa = sb("wa", [P, 2, 2])
        ones = sb("ones", [P, P])
        wa2rep = [sb(f"wa2rep{l}", [P, P]) for l in range(2)]
        gcol = sb("gcol", [P, 1])
        bcol = sb("bcol", [P, 1])
        b1col = sb("b1col", [P, E0 * C0])
        b1row = sb("b1row", [E0 * C0, P])
        wr_sb = sb("wr_sb", [P, E0])
        brow = sb("brow", [P, E0])
        rw_row = sb("rw_row", [E1, P])
        rwT = sb("rwT", [P, E1])
        rbrow = sb("rbrow", [P, E1])
        iota_i = sb("iota_i", [P, E1], I32)
        iota = sb("iota", [P, E1])
        spare = sb("spare", [P, 1])
        eps = sb("eps", [P, G])
        neghalf = sb("neghalf", [P, G])
        w1hi = sb("w1hi", [P, E0 * H0], F32R)
        w1lo = sb("w1lo", [P, E0 * H0], F32R)
        w2hi = sb("w2hi", [P, E0 * C0, P], F32R)
        w2lo = sb("w2lo", [P, E0 * C0, P], F32R)
        b2col = sb("b2col", [P, E0])
        b2row = sb("b2row", [E0, P])
        v1hi = sb("v1hi", [P, E1 * H1], F32R)
        v1lo = sb("v1lo", [P, E1 * H1], F32R)
        v2hi = sb("v2hi", [P, NCH, P], F32R)
        v2lo = sb("v2lo", [P, NCH, P], F32R)
        c2 = sb("c2", [64, P], F32R)
        sel = sb("sel", [WCOL, E1 * H1], F32R)

        x0 = [sb(f"x0_{p}", [P, G, P]) for p in range(2)]
        x0k = [sb(f"x0k_{p}", [P, G, P]) for p in range(2)]
        x1 = [sb(f"x1_{p}", [P, G, P]) for p in range(2)]
        x2 = [sb(f"x2_{p}", [P, G, P]) for p in range(2)]
        prT = {k: sb(f"prT{k}", [P, T]) for k in "BF"}
        st = {k: sb(f"st{k}", [P, G, 6]) for k in "ACEF"}
        mv = {k: sb(f"mv{k}", [P, G, 2]) for k in "ACEF"}
        ve = {k: sb(f"ve{k}", [P, G]) for k in "ACEF"}
        rs = {k: sb(f"rs{k}", [P, G]) for k in "ACEF"}
        v2t = sb("v2t", [P, 4, G])
        xn = {k: sb(f"xn{k}", [P, G, P]) for k in "AE"}
        xn["C"], xn["F"] = xn["A"], xn["E"]
        xnT = {k: sb(f"xnT{k}", [P, T]) for k in "ACEF"}
        hg = {k: [sb(f"hg{k}{p}", [P, G, P]) for p in range(2)] for k in "AE"}
        s1 = {k: sb(f"s1{k}", [P, G]) for k in "AE"}
        tt = {k: sb(f"tt{k}", [P, G, P]) for k in "AE"}
        em = {k: sb(f"em{k}", [P, G]) for k in "AE"}
        sc = {k: sb(f"sc{k}", [P, G, P]) for k in "AE"}
        pr = {k: sb(f"pr{k}", [P, G, P]) for k in "BF"}
        rsum = {k: sb(f"rsum{k}", [P, G]) for k in "BF"}
        rinv = {k: sb(f"rinv{k}", [P, G]) for k in "BF"}
        z = {k: sb(f"z{k}", [P, G, P]) for k in "BF"}
        zneg = sb("zneg", [P, G, P])
        xhi = {k: [sb(f"xhi{k}{p}", [P, T], F32R) for p in range(2)] for k in "CF"}
        xlo = {k: [sb(f"xlo{k}{p}", [P, T], F32R) for p in range(2)] for k in "CF"}
        lg = {"C": sb("lgC", [P, G, E0]), "F": sb("lgF", [P, G, E1])}
        top = {k: sb(f"top{k}", [P, G, 8]) for k in "CF"}
        idx = {k: sb(f"idx{k}", [P, G, 8], U32) for k in "CF"}
        idf = {k: sb(f"idf{k}", [P, G, 2]) for k in "CF"}
        dif = sb("dif", [P, G])
        th = sb("th", [P, G])
        w01 = sb("w01", [P, 2, G])
        oh2 = sb("oh2", [P, 2, G, E0])
        ohw = sb("ohw", [P, 2, G, E0])
        wb = [sb(f"wb{s}", [P, T]) for s in range(NWB)]
        x1n = sb("x1n", [P, G, P])
        wo = sb("wo", [P, G, P])
        woT = [sb(f"woT{p}", [WCOL, T], F32R) for p in range(2)]
        wT = sb("wT", [P, T])
        with ExitStack() as early:
            def raw(name, shape, dt=F32):
                return early.enter_context(nc.sbuf_tensor(name, shape, dt))

            v1raw = raw("v1raw", [P, E1 * H1])
            v2raw = raw("v2raw", [P, NCH, P])
            selraw = raw("selraw", [WCOL, E1 * H1])
            selhi = raw("selhi", [WCOL, E1 * H1], F32R)
            c2raw = raw("c2raw", [64, P])
            c2hi = raw("c2hi", [64, P], F32R)
            w1raw = raw("w1raw", [P, E0 * H0])
            w2raw = raw("w2raw", [P, E0 * C0, P])
            arow = raw("arow", [P, 2, 2, P])
            wprod = raw("wprod", [P, 2, 2, P])
            adj_i = raw("adj_i", [P, P], I32)
            adj_f = raw("adj_f", [P, P])
            adj_m = raw("adj_m", [P, 2, P])
        x3 = [sb(f"x3_{p}", [P, G, P]) for p in range(2)]
        fin = [sb(f"fin{p}", [P, G, P]) for p in range(2)]
        rhi = [sb(f"rhi{s}", [P, T], F32R) for s in range(2)]
        rlo = [sb(f"rlo{s}", [P, T], F32R) for s in range(2)]
        oT = sb("oT", [P, T])
        hid = [[sb(f"hid{s}{c}", [P, T]) for c in range(C0)] for s in range(2)]
        hhi = [[sb(f"hhi{s}{c}", [P, T], F32R) for c in range(C0)] for s in range(2)]
        hlo = [[sb(f"hlo{s}{c}", [P, T], F32R) for c in range(C0)] for s in range(2)]
        ym = [sb(f"ym{s}", [P, T]) for s in range(2)]
        acc = [sb(f"acc{p}", [P, T]) for p in range(2)]

        ZB = [pb("Z0"), pb("Z1")]
        YB = pb("Y")
        OB = pb("O")
        TP0 = pb("TP0")
        TP1 = pb("TP1")
        HB = pb("H")
        SB = pb("S")
        TPB = dict(A=TP0, B=TP0, C=TP0, E=TP1, F=TP1)

        def g4(t):
            return t[:, :].rearrange("p (g f) -> p g f", g=G)

        def each(body):
            def run(eng, before={}):
                for i in range(FIRST):
                    if i in before:
                        before[i]()
                    body(i // 2, i % 2)
                with eng.Fori(FIRST // 2, NGROUP // 2) as j:
                    for p in range(2):
                        body(j, p)
                for i in range(NGROUP, NITER):
                    body(i // 2, i % 2)
            return run

        def h3(k):
            return (HB if k == "A" else TP1)[:, 0:(G - 1) * (P + 1)].rearrange("p (g f) -> p g f", g=G - 1)

        def h4(k):
            n = "AE".index(k) * (P + 1)
            return TP0[:, n:n + P + 1]

        def half_bank(s, c):
            return ZB[(s + c) % 2]

        def chunk_bank(s):
            return ZB[s % 2]

        def l2_done(eng, g, s):
            if s >= 2:
                after(eng, "d_l2", g, E0, s - 1)
            else:
                after(eng, "d_l2", g.before(1), E0, E0 + s - 1)

        def m2_done(eng, g, s):
            if s >= 2:
                after(eng, "m_l2", g, NCH, s - 1)
            else:
                after(eng, "m_l2", g.before(1), NCH, NCH + s - 1)

        NGRAPHIN, NMIXIN, NMIX2IN = 5, 10, 4
        wrows = nc.dram_tensor("wrows", [2, E0, T], F32, kind="Internal").ap()
        xg = x.rearrange("(n g) t f -> n t g f", g=G)
        og = out.rearrange("(n g) t f -> n t g f", g=G)
        block = ctx.enter_context(nc.Block())

        @block.sync
        def _(sp):
            def graph_const(dst, src):
                sp.dma_start(dst, src).then_inc(sem("graph_in"), 16)

            def mix_const(dst, src):
                sp.dma_start(dst, src).then_inc(sem("mix_in"), 16)

            def mix2_const(dst, src):
                sp.dma_start(dst, src).then_inc(sem("mix2_in"), 16)

            graph_const(adj_i[:, :], adj)
            graph_const(Wg[0][:, 0:P], W_0)
            graph_const(Wg[1][:, 0:P], W_1)
            for l, a in enumerate((a_0, a_1)):
                graph_const(arow[:, l, :, :], a.rearrange("(o k f) u -> o k (f u)", o=1, k=2).broadcast_to([P, 2, P]))

            def load_first():
                mix_const(b1row[:, :], b1_0.rearrange("e (c p) -> (e c) p", c=C0))
                mix_const(b2row[:, :], b2_0)
                mix_const(rw_row[:, :], rw)
                mix_const(gcol[:, :], gamma.rearrange("(p u) -> p u", u=1))
                mix_const(bcol[:, :], beta.rearrange("(p u) -> p u", u=1))
                mix_const(wr_sb[:, :], Wr)
                mix_const(brow[:, :], br.rearrange("(u e) -> u e", u=1).broadcast_to([P, E0]))
                mix_const(rbrow[:, :], rb.rearrange("(u e) -> u e", u=1).broadcast_to([P, E1]))
                mix_const(w1raw[:, :].rearrange("p (e h) -> p e h", e=E0), W1_0.rearrange("e d h -> d e h"))
                mix_const(w2raw[:, :, :], W2_0.rearrange("e (c p) d -> p (e c) d", c=C0))

            def load_second():
                mix2_const(v1raw[:, :].rearrange("p (e h) -> p e h", e=E1), W1_1.rearrange("e d h -> d e h"))
                mix2_const(v2raw[:, :, :], W2_1.rearrange("(c q) h d -> (q h) c d", c=NCH))
                for r in range(2):
                    mix2_const(c2raw[32 * r:32 * r + 32, :], b2_1)
                for r in range(2):
                    sp.dma_start(selraw[32 * r:32 * r + 32, :].rearrange("e (f h) -> e f h", f=E1),
                                 b1_1.rearrange("e (u h) -> e u h", u=1).broadcast_to([E1, E1, H1])).then_inc(sem("b1_in"), 16)

            def load(g):
                if g.before(2).live():
                    sp.wait_ge(sem(f"kept{g.par}"), 16 * g.half)
                sp.dma_start(x0[g.par][:, :, :], xg[g.n]).then_inc(sem(f"x0_in{g.par}"), 16)

            def spread(g, e):
                if e == 0:
                    after(sp, "w_out", g, 16, 16)
                elif e >= NWB:
                    after(sp, "ym", g, E0, e - NWB + 1)
                elif e >= 2:
                    after(sp, "ym", g.before(1), E0, E0 + e - NWB + 1)
                sp.dma_start(wb[e % NWB][:, :], wrows[g.par, e:e + 1, :].broadcast_to([P, T])).then_inc(sem(f"wb_in{e % NWB}"), 16)

            @each
            def body(j, p):
                g = At(j, p, LAG["A"])
                if g.live():
                    load(g)
                D = At(j, p, LAG["D"])
                if D.live():
                    after(sp, "woT", At(j, p, LAG["D"], NTURN))
                    sp.dma_start(wrows[D.par, :, :], wT[WCOL:WCOL + E0, :]).then_inc(sem("w_out"), 16)
                    for e in range(NWB):
                        spread(D, e)
                g = At(j, p, LAG["a"])
                if g.live():
                    if g.before(2).live():
                        after(sp, "x1", g.before(2))
                    else:
                        after(sp, "xnA", g)
                    sp.dma_start(x0k[g.par][:, :, :], x0[g.par][:, :, :]).then_inc(sem(f"kept{g.par}"), 16)
                if D.live():
                    spread(D, NWB)
                g = At(j, p, LAG["O"])
                if g.live():
                    after(sp, "fin", g)
                    sp.dma_start(og[g.n], fin[g.par][:, :, :]).then_inc(sem(f"stored{g.par}"), 16)
                if D.live():
                    for e in range(NWB + 1, E0):
                        spread(D, e)

            body(sp, {3: load_first, 5: load_second})
            for p in range(2):
                sp.wait_ge(sem(f"stored{p}"), 16 * (NGROUP // 2))

        @block.gpsimd
        def _(pool):
            pool.memset(neghalf[:, :], -0.5)
            pool.memset(eps[:, :], EPS)
            pool.memset(ident[:, :], 0.0).then_inc(sem("zeroed"), 1)
            pool.wait_ge(sem("zeroed"), 1)
            pool.affine_select(out=ident[:, :], in_=ident[:, :], compare_op=ALU.not_equal, fill=1.0, base=0,
                               pattern=[[-1, P]], channel_multiplier=1).then_inc(sem("ident"), 1)
            pool.iota(iota_i[:, :], pattern=[[1, E1]], base=0, channel_multiplier=0).then_inc(sem("iota"), 1)
            def bias_rows():
                pool.wait_ge(sem("b1_in"), 32)
                pool.wait_ge(sem("masked"), 1)
                pool.wait_ge(sem("iota"), 1)
                for r in range(3):
                    if r:
                        pool.wait_ge(sem("sel_raw"), r)
                    part = selraw[32 * r:32 * r + 32, :].rearrange("e (f h) -> e f h", f=E1)
                    pool.affine_select(out=part, in_=part, compare_op=ALU.is_equal, fill=0.0, base=0,
                                       pattern=[[-1, E1], [0, H1]], channel_multiplier=1).then_inc(sem("sel_raw"), 1)
                pool.wait_ge(sem("sel_raw"), 3)

            def first_lo():
                pool.wait_ge(sem("w_hi"), 2)
                pool.tensor_tensor(w2lo[:, :, :], w2raw[:, :, :], w2hi[:, :, :].bitcast(F32),
                                   ALU.subtract).then_inc(sem("w2_lo"), 1)

            def second_lo():
                pool.wait_ge(sem("v_hi"), 1)
                pool.tensor_tensor(v1lo[:, :], v1raw[:, :], v1hi[:, :].bitcast(F32), ALU.subtract)
                pool.tensor_tensor(v2lo[:, :, :], v2raw[:, :, :], v2hi[:, :, :].bitcast(F32),
                                   ALU.subtract).then_inc(sem("v_lo"), 1)

            def rstd(k, g):
                after(pool, f"moments{k}", g)
                pool.tensor_tensor(ve[k][:, :], mv[k][:, :, 1], eps[:, :], ALU.add).then_inc(sem(f"var_eps{k}"), 1)
                after(pool, f"var_eps{k}", g)
                if k != "C":
                    after(pool, f"xn{k}", g.before(1))
                    pool.tensor_tensor(rs[k][:, :], ve[k][:, :], neghalf[:, :], ALU.pow).then_inc(sem(f"rstd{k}"), 1)
                    return
                c = [v2t[:, n, :] for n in range(4)]
                pool.tensor_tensor(c[0], ve[k][:, :], neghalf[:, :], ALU.pow).then_inc(sem("second"), 1)
                after(pool, "second", g, 5, 1)
                pool.tensor_tensor(c[1], c[0], c[0], ALU.mult).then_inc(sem("second"), 1)
                after(pool, "second", g, 5, 2)
                pool.tensor_tensor(c[2], c[1], mv[k][:, :, 1], ALU.mult).then_inc(sem("second"), 1)
                after(pool, "second", g, 5, 3)
                pool.tensor_tensor(c[1], c[2], eps[:, :], ALU.add).then_inc(sem("second"), 1)
                after(pool, "second", g, 5, 4)
                pool.tensor_tensor(c[3], c[1], neghalf[:, :], ALU.pow).then_inc(sem("second"), 1)
                after(pool, "second", g, 5, 5)
                after(pool, f"xn{k}", g.before(1))
                pool.tensor_tensor(rs[k][:, :], c[0], c[3], ALU.mult).then_inc(sem(f"rstd{k}"), 1)

            def round_rest(k, g):
                after(pool, f"xhi{k}", g)
                user, n = ("d_l1", E0 * C0) if k == "C" else ("m_l1", NCH)
                after(pool, user, g.before(2), n, n)
                pool.tensor_tensor(xlo[k][g.par][:, :], xnT[k][:, :], xhi[k][g.par][:, :].bitcast(F32),
                                   ALU.subtract).then_inc(sem(f"xlo{k}"), 1)

            @each
            def body(j, p):
                at = stages(j, p)
                for s in range(SLOTS):
                    g = at["D"]
                    if g.live():
                        after(pool, "hhi1", g, E0, s + 1)
                        l2_done(pool, g, s)
                        pool.tensor_tensor(hlo[s % 2][1][:, :], hid[s % 2][1][:, :], hhi[s % 2][1][:, :].bitcast(F32),
                                           ALU.subtract).then_inc(sem("hlo1"), 1)
                    for k, slot in (("C", 2), ("F", 4), ("E", 5)):
                        if s == slot and at[k].live():
                            rstd(k, at[k])
                    if s == 6 and at["F"].live():
                        round_rest("F", at["F"])
                    g, e = (at["D"].before(1), SLOTS - 1) if s == 0 else (at["D"], s - 1)
                    if g.live() and e >= 1:
                        after(pool, "ym", g, SLOTS, e + 1)
                        if e >= 2:
                            after(pool, "ysum", g, SLOTS - 1, e - 1)
                        to = acc[g.par]
                        pool.tensor_tensor(to[:, :], to[:, :], ym[e % 2][:, :], ALU.add).then_inc(sem("ysum"), 1)
                    if s == 0 and at["A"].live():
                        rstd("A", at["A"])
                    if s == 5 and at["a"].live():
                        g = at["a"]
                        after(pool, "rowmaxA", g)
                        pool.tensor_tensor(sc["A"][:, :, :], sc["A"][:, :, :], em["A"][:, :].unsqueeze(2).broadcast_to([P, G, P]),
                                           ALU.subtract).then_inc(sem("scoreA"), 1)
                    if s == 6 and at["C"].live():
                        round_rest("C", at["C"])
                    g = at["C"]
                    if s == 3 and g.live():
                        after(pool, "x1", g)
                        after(pool, "x2", g.before(2))
                        pool.tensor_tensor(x1[g.par][:, :, :], x1n[:, :, :], ones[:, :].unsqueeze(1).broadcast_to([P, G, P]),
                                           ALU.mult).then_inc(sem("x1c"), 1)

            body(pool, {4: first_lo, 6: bias_rows, 7: second_lo})

        @block.scalar
        def _(act):
            def xT_out(k, g):
                after(act, f"xn_ps{k}", g)
                if k in "AE":
                    after(act, f"s_ps{k}", g.before(1))
                else:
                    after(act, f"lg_ps{k}", g.before(1))
                    after(act, f"xlo{k}", g.before(1))
                if k == "C":
                    act.activation(xnT[k][:, :], TPB[k][:, :], ACT.Identity, scale=gcol[:, 0:1],
                                   bias=bcol[:, 0:1]).then_inc(sem(f"xnT{k}"), 1)
                else:
                    act.activation(xnT[k][:, :], TPB[k][:, :], ACT.Copy).then_inc(sem(f"xnT{k}"), 1)

            def round_rows(k, g):
                after(act, f"xnT{k}", g)
                user, n = ("d_l1", E0 * C0) if k == "C" else ("m_l1", NCH)
                after(act, user, g.before(2), n, n)
                act.activation(xhi[k][g.par][:, :], xnT[k][:, :], ACT.Copy).then_inc(sem(f"xhi{k}"), 1)

            def h_out(k, g):
                after(act, f"h_ps{k}", g)
                after(act, f"att_ps{'B' if k == 'A' else 'F'}", g.before(2))
                act.activation(hg[k][g.par][:, 0:G - 1, :], h3(k)[:, :, 0:P], ACT.Copy)
                act.activation(hg[k][g.par][:, G - 1, :], h4(k)[:, 0:P], ACT.Copy).then_inc(sem(f"h{k}"), 1)

            def prT_out(k, g):
                after(act, f"pr_ps{k}", g)
                after(act, f"att_ps{k}", g.before(1))
                act.activation(prT[k][:, :], TP1[:, :], ACT.Copy).then_inc(sem(f"prT{k}"), 1)

            def exps(at):
                for k, src in (("F", "E"), ("B", "A")):
                    g = at[k]
                    if g.live():
                        after(act, f"score{src}", g)
                        after(act, f"pr_ps{k}", g.before(1))
                        after(act, f"rsum{k}", g.before(1))
                        act.activation(pr[k][:, :, :], sc[src][:, :, :], ACT.Exp).then_inc(sem(f"pr{k}"), 1)
                g = at["C"]
                if g.live():
                    after(act, "zneg", g)
                    act.activation(zneg[:, :, :], zneg[:, :, :], ACT.Exp).then_inc(sem("eneg"), 1)

            @each
            def body(j, p):
                at = stages(j, p)
                for s in range(SLOTS):
                    g = at["D"]
                    if g.live():
                        for c in range(C0):
                            n = C0 * s + c
                            after(act, "d_l1", g, E0 * C0, n + 1)
                            if s >= 2:
                                after(act, f"hlo{c}", g, E0, s - 1)
                            else:
                                after(act, f"hlo{c}", g.before(1), E0, E0 + s - 1)
                            act.activation(hid[s % 2][c][:, :], half_bank(s, c)[:, :], ACT.Gelu,
                                           bias=b1col[:, n:n + 1]).then_inc(sem("gelu"), 1)
                        for c in range(C0):
                            after(act, "gelu", g, E0 * C0, C0 * s + c + 1)
                            l2_done(act, g, s)
                            act.activation(hhi[s % 2][c][:, :], hid[s % 2][c][:, :], ACT.Copy).then_inc(sem(f"hhi{c}"), 1)
                    g = at["M"]
                    if g.live():
                        after(act, "m_l1", g, NCH, s + 1)
                        m2_done(act, g, s)
                        act.activation(rhi[s % 2][:, :], chunk_bank(s)[:, :], ACT.Relu).then_inc(sem("relu"), 1)
                    g = at["M"].before(1)
                    if s == 0 and g.live():
                        after(act, "m_l2", g, NCH, NCH)
                        after(act, "out_ps", g.before(1))
                        act.activation(oT[:, :], OB[:, :], ACT.Relu).then_inc(sem("oT"), 1)
                    if s == 0:
                        exps(at)
                    if s == 1:
                        for k in "ae":
                            after(act, f"s1{k.upper()}", at[k])
                        for k in "ae":
                            if at[k].live():
                                h_out(k.upper(), at[k])
                    if s == 2 and at["A"].live():
                        xT_out("A", at["A"])
                    if s == 2 and at["F"].live():
                        prT_out("F", at["F"])
                    if s == 4:
                        if at["C"].live():
                            xT_out("C", at["C"])
                        if at["B"].live():
                            prT_out("B", at["B"])
                    if s == 5:
                        if at["C"].live():
                            round_rows("C", at["C"])
                        if at["F"].live():
                            xT_out("F", at["F"])
                    if s == 6 and at["F"].live():
                        round_rows("F", at["F"])
                    if s == 6 and at["C"].live():
                        after(act, "dif", at["C"])
                        act.activation(th[:, :], dif[:, :], ACT.Tanh, scale=0.5).then_inc(sem("tanh"), 1)
                    if s == 7:
                        if at["E"].live():
                            xT_out("E", at["E"])
                        g = at["W"]
                        if g.live():
                            after(act, "wo_ps", g)
                            after(act, "w_out", at["C"].before(1), 16, 16)
                            after(act, "m_l1", at["F"].before(2), NCH, NCH)
                            after(act, "m_l2", at["F"].before(2), NCH, NCH)
                            if at["C"].live():
                                act.activation(wT[WCOL:WCOL + E0, :], TP0[WCOL:WCOL + E0, :], ACT.Copy)
                            act.activation(woT[g.par][0:WCOL, :], TP0[0:WCOL, :], ACT.Copy).then_inc(sem("woT"), 1)

            def round_weights():
                act.wait_ge(sem("mix_in"), 16 * NMIXIN)
                act.activation(w1hi[:, :], w1raw[:, :], ACT.Copy).then_inc(sem("w_hi"), 1)
                act.activation(w2hi[:, :, :], w2raw[:, :, :], ACT.Copy).then_inc(sem("w_hi"), 1)

            def round_second():
                act.wait_ge(sem("mix2_in"), 16 * NMIX2IN)
                act.activation(v1hi[:, :], v1raw[:, :], ACT.Copy)
                act.activation(v2hi[:, :, :], v2raw[:, :, :], ACT.Copy).then_inc(sem("v_hi"), 1)

            def columns():
                act.wait_ge(sem("cols"), 1)

            body(act, {3: round_weights, 4: columns, 6: round_second})

        @block.vector
        def _(dve):
            steps = [0]

            def link(ins):
                steps[0] += 1
                ins.then_inc(sem("setup_v"), 1)
                dve.wait_ge(sem("setup_v"), steps[0])

            dve.memset(ones[:, :], 1.0)
            dve.memset(wo[:, :, :], 0.0)
            dve.wait_ge(sem("graph_in"), 16 * NGRAPHIN)
            dve.tensor_copy(adj_f[:, :], adj_i[:, :])
            link(dve.tensor_tensor(wprod[:, 0, :, :], Wg[0][:, 0:P].unsqueeze(1).broadcast_to([P, 2, P]), arow[:, 0, :, :], ALU.mult))
            dve.tensor_scalar(adj_m[:, 0, :], adj_f[:, :], 0.0, 1.0, ALU.is_gt, ALU.subtract)
            dve.tensor_scalar(adj_m[:, 1, :], adj_f[:, :], 0.0, 1.0, ALU.not_equal, ALU.subtract)
            link(dve.tensor_tensor(wprod[:, 1, :, :], Wg[1][:, 0:P].unsqueeze(1).broadcast_to([P, 2, P]), arow[:, 1, :, :], ALU.mult))
            for l in range(2):
                dve.tensor_scalar(mask[l][:, :], adj_m[:, l, :], -MASKED, None, ALU.mult)
            link(dve.reduce_sum(wa[:, :, :], wprod[:, :, :, :], AX.X))
            for l in range(2):
                dve.tensor_copy(Wg[l][:, P:P + 1], wa[:, l, 0:1])
                dve.tensor_scalar(wa2rep[l][:, :], ones[:, :], wa[:, l, 1:2], None, ALU.mult)
            dve.wait_ge(sem("ident"), 1)
            dve.tensor_copy(identb[:, :], ident[:, :]).then_inc(sem("graph_consts"), 1)

            def mask_rows():
                dve.memset(selraw[64:WCOL, :], MASKED).then_inc(sem("masked"), 1)
                dve.wait_ge(sem("iota"), 1)
                dve.tensor_copy(iota[:, :], iota_i[:, :])

            def columns():
                dve.wait_ge(sem("cols_ps"), 1)
                dve.tensor_copy(rwT[:, :], YB[:, 0:E1])
                dve.tensor_copy(b2col[:, :], YB[:, E1 + E0 * C0:E1 + E0 * C0 + E0])
                dve.tensor_copy(b1col[:, :], YB[:, E1:E1 + E0 * C0]).then_inc(sem("cols"), 1)

            def first_weights():
                dve.wait_ge(sem("w_hi"), 1)
                dve.tensor_tensor(w1lo[:, :], w1raw[:, :], w1hi[:, :].bitcast(F32), ALU.subtract).then_inc(sem("w1_lo"), 1)
                columns()

            def biases():
                dve.wait_ge(sem("sel_raw"), 3)
                dve.wait_ge(sem("mix2_in"), 16 * NMIX2IN)
                dve.tensor_copy(c2hi[:, :], c2raw[:, :])
                link(dve.tensor_copy(selhi[:, :], selraw[:, :]))
                dve.tensor_copy(c2[0:32, :], c2hi[0:32, :].bitcast(F32))
                dve.tensor_tensor(c2[32:64, :], c2raw[32:64, :], c2hi[32:64, :].bitcast(F32), ALU.subtract)
                dve.tensor_copy(sel[0:32, :], selhi[0:32, :].bitcast(F32))
                dve.tensor_tensor(sel[32:64, :], selraw[32:64, :], selhi[32:64, :].bitcast(F32), ALU.subtract)
                dve.tensor_copy(sel[64:WCOL, :], selhi[64:WCOL, :].bitcast(F32)).then_inc(sem("biases"), 1)

            def biases_and_weights():
                biases()
                dve.wait_ge(sem("v_lo"), 1)

            def stats(k, g, xin):
                for n in range(G):
                    last = dve.bn_stats(st[k][:, n, :], xin[:, n, :])
                last.then_inc(sem(f"stats{k}"), 1)
                after(dve, f"stats{k}", g)
                after(dve, f"rstd{k}", g.before(1))
                settle()
                for n in range(G):
                    last = dve.bn_aggr(mv[k][:, n, :], st[k][:, n, :])
                last.then_inc(sem(f"moments{k}"), 1)

            def norm(k, g, xin):
                after(dve, f"rstd{k}", g)
                after(dve, f"xn_ps{k}", g.before(1))
                for n in range(G):
                    last = dve.tensor_scalar(xn[k][:, n, :], xin[:, n, :], mv[k][:, n, 0:1], rs[k][:, n:n + 1],
                                             ALU.subtract, ALU.mult)
                last.then_inc(sem(f"xn{k}"), 1)

            def s1_out(k, g):
                after(dve, f"h_ps{k}", g)
                after(dve, f"raw{k}", g.before(1))
                dve.tensor_copy(s1[k][:, 0:G - 1], h3(k)[:, :, P])
                dve.tensor_copy(s1[k][:, G - 1:G], h4(k)[:, P:P + 1]).then_inc(sem(f"s1{k}"), 1)

            def raw_scores(k, g):
                after(dve, f"s1{k}", g)
                after(dve, f"s_ps{k}", g)
                after(dve, f"leaky{k}", g.before(1))
                dve.tensor_tensor(tt[k][:, :, :], g4(SB), s1[k][:, :].unsqueeze(2).broadcast_to([P, G, P]),
                                  ALU.add).then_inc(sem(f"raw{k}"), 1)

            def scores(k, g):
                l = "AE".index(k)
                after(dve, f"raw{k}", g)
                after(dve, f"pr{'B' if k == 'A' else 'F'}", g.before(1))
                dve.scalar_tensor_tensor(sc[k][:, :, :], tt[k][:, :, :], SLOPE[l], tt[k][:, :, :], ALU.mult,
                                         ALU.max).then_inc(sem(f"leaky{k}"), 1)
                after(dve, f"leaky{k}", g)
                dve.reduce_max(em[k][:, :], sc[k][:, :, :], AX.X).then_inc(sem(f"rowmax{k}"), 1)
                if k == "A":
                    return
                after(dve, f"rowmax{k}", g)
                dve.tensor_tensor(sc[k][:, :, :], sc[k][:, :, :], em[k][:, :].unsqueeze(2).broadcast_to([P, G, P]),
                                  ALU.subtract).then_inc(sem(f"score{k}"), 1)

            def row_sums(k, g):
                after(dve, f"pr{k}", g)
                dve.reduce_sum(rsum[k][:, :], pr[k][:, :, :], AX.X).then_inc(sem(f"rsum{k}"), 1)
                after(dve, f"rsum{k}", g)
                after(dve, f"z{k}", g.before(1))
                dve.reciprocal(rinv[k][:, :], rsum[k][:, :]).then_inc(sem(f"rinv{k}"), 1)

            def attended(k, g):
                after(dve, f"rinv{k}", g)
                after(dve, f"att_ps{k}", g)
                if k == "B":
                    after(dve, "x1a", g.before(1))
                dve.tensor_tensor(z[k][:, :, :], g4(HB), rinv[k][:, :].unsqueeze(2).broadcast_to([P, G, P]),
                                  ALU.mult).then_inc(sem(f"z{k}"), 1)
                after(dve, f"z{k}", g)

            def logits(k, g, bias, n):
                after(dve, f"lg_ps{k}", g)
                dve.tensor_tensor(lg[k][:, :, :], SB[:, 0:G * n].rearrange("p (g e) -> p g e", g=G),
                                  bias[:, :].unsqueeze(1).broadcast_to([P, G, n]), ALU.add).then_inc(sem(f"lg{k}"), 1)
                after(dve, f"lg{k}", g)
                settle()
                for q in range(G):
                    last = dve.max(top[k][:, q, :], lg[k][:, q, :])
                last.then_inc(sem(f"top{k}"), 1)
                after(dve, f"top{k}", g)
                settle()
                for q in range(G):
                    last = dve.max_index(idx[k][:, q, :], top[k][:, q, :], lg[k][:, q, :])
                last.then_inc(sem(f"idx{k}"), 1)
                after(dve, f"idx{k}", g)
                dve.tensor_copy(idf[k][:, :, :], idx[k][:, :, 0:2]).then_inc(sem(f"idf{k}"), 1)

            @each
            def body(j, p):
                at = stages(j, p)
                A, B, C, D, E, F, M, O, W = (at[k] for k in "ABCDEFMOW")
                for s in range(SLOTS):
                    if s == 5 and F.live():
                        after(dve, "xn_psE", E.before(1))
                        norm("F", F, x3[F.par])
                    if s == 5 and at["a"].live():
                        scores("A", at["a"])
                    if s == 7 and E.live():
                        after(dve, "xn_psF", F)
                        norm("E", E, x2[E.par])
                    if s == 1:
                        after(dve, "h_psE", at["e"])
                        for k in "ae":
                            if at[k].live():
                                s1_out(k.upper(), at[k])
                        if at["a"].live():
                            raw_scores("A", at["a"])
                    if D.live():
                        after(dve, "hhi0", D, E0, s + 1)
                        l2_done(dve, D, s)
                        dve.tensor_tensor(hlo[s % 2][0][:, :], hid[s % 2][0][:, :], hhi[s % 2][0][:, :].bitcast(F32),
                                          ALU.subtract).then_inc(sem("hlo0"), 1)
                    if M.live():
                        after(dve, "relu", M, NCH, s + 1)
                        m2_done(dve, M, s)
                        dve.scalar_tensor_tensor(rlo[s % 2][:, :], chunk_bank(s)[:, :], 0.0,
                                                 rhi[s % 2][:, :].bitcast(F32), ALU.max,
                                                 ALU.subtract).then_inc(sem("rlo"), 1)
                    g, e = (D.before(1), SLOTS - 1) if s == 0 else (D, s - 1)
                    if g.live():
                        after(dve, "d_l2", g, E0, e + 1)
                        after(dve, f"wb_in{e % NWB}", g, 32, 16 * (e // NWB + 1))
                        if e == 0:
                            after(dve, "y_ps", g.before(2))
                            to = acc[g.par]
                        else:
                            to = ym[e % 2]
                            if e >= 3:
                                after(dve, "ysum", g, SLOTS - 1, e - 2)
                            else:
                                after(dve, "ysum", g.before(1), SLOTS - 1, SLOTS - 1 + min(e - 2, 0))
                        dve.scalar_tensor_tensor(to[:, :], YB[:, :], b2col[:, e:e + 1], wb[e % NWB][:, :], ALU.add,
                                                 ALU.mult).then_inc(sem("ym"), 1)
                    if s == 0 and A.live():
                        dve.wait_ge(sem(f"x0_in{A.par}"), 16 * (A.half + 1))
                        stats("A", A, x0[A.par])
                        after(dve, "xn_psC", C.before(1))
                        norm("A", A, x0[A.par])
                    if s == 1:
                        if at["e"].live():
                            raw_scores("E", at["e"])
                        if C.live():
                            after(dve, "x1c", C.before(1))
                            dve.wait_ge(sem(f"kept{C.par}"), 16 * (C.half + 1))
                            dve.scalar_tensor_tensor(x1n[:, :, :], z["B"][:, :, :], 0.0, x0k[C.par][:, :, :], ALU.max,
                                                     ALU.add).then_inc(sem("x1a"), 1)
                            after(dve, "x1a", C)
                            after(dve, "eneg", C)
                            dve.scalar_tensor_tensor(x1n[:, :, :], zneg[:, :, :], 1.0, x1n[:, :, :],
                                                     ALU.subtract, ALU.add).then_inc(sem("x1"), 1)
                            after(dve, "x1", C)
                            stats("C", C, x1n)
                    if s == 2:
                        if F.live():
                            row_sums("F", F)
                        if B.live():
                            row_sums("B", B)
                        if O.live():
                            after(dve, "out_ps", O)
                            if O.before(2).live():
                                dve.wait_ge(sem(f"stored{O.par}"), 16 * O.half)
                            dve.tensor_tensor(fin[O.par][:, :, :], g4(TP0), x3[O.par][:, :, :], ALU.add).then_inc(sem("fin"), 1)
                    if s == 3:
                        if F.live():
                            attended("F", F)
                            after(dve, "fin", F.before(2))
                            dve.scalar_tensor_tensor(x3[F.par][:, :, :], z["F"][:, :, :], 0.0, x2[F.par][:, :, :], ALU.max,
                                                     ALU.add).then_inc(sem("x3"), 1)
                        if C.live():
                            after(dve, "xn_psA", A)
                            norm("C", C, x1n)
                        if E.live():
                            after(dve, "y_ps", E)
                            after(dve, "x3", E.before(2))
                            dve.tensor_tensor(x2[E.par][:, :, :], g4(TP0), x1[E.par][:, :, :], ALU.add).then_inc(sem("x2"), 1)
                        if F.live():
                            after(dve, "x3", F)
                            stats("F", F, x3[F.par])
                    if s == 4:
                        if E.live():
                            after(dve, "x2", E)
                            stats("E", E, x2[E.par])
                    if s == 5:
                        if C.live():
                            logits("C", C, brow, E0)
                            after(dve, "tanh", C.before(1))
                            dve.tensor_tensor(dif[:, :], top["C"][:, :, 0], top["C"][:, :, 1], ALU.subtract).then_inc(sem("dif"), 1)
                            after(dve, "idfC", C)
                            for n in range(2):
                                dve.tensor_tensor(oh2[:, n, :, :], iota[:, 0:E0].unsqueeze(1).broadcast_to([P, G, E0]),
                                                  idf["C"][:, :, n:n + 1].broadcast_to([P, G, E0]),
                                                  ALU.is_equal).then_inc(sem("oh2"), 1)
                    if s == 6:
                        if F.live():
                            logits("F", F, rbrow, E1)
                            after(dve, "idfF", F)
                            after(dve, "wo_ps", W.before(1))
                            for r in range(3):
                                op = ALU.not_equal if r == 2 else ALU.is_equal
                                last = dve.tensor_tensor(wo[:, :, r * E1:(r + 1) * E1],
                                                         iota[:, :].unsqueeze(1).broadcast_to([P, G, E1]),
                                                         idf["F"][:, :, 0:1].broadcast_to([P, G, E1]), op)
                            last.then_inc(sem("ohc"), 1)
                        if C.live():
                            after(dve, "tanh", C)
                            dve.tensor_scalar(w01[:, 0, :], th[:, :], 0.5, 0.5, ALU.mult, ALU.add)
                            dve.tensor_scalar(w01[:, 1, :], th[:, :], -0.5, 0.5, ALU.mult, ALU.add).then_inc(sem("w01"), 1)
                            after(dve, "w01", C)
                            after(dve, "oh2", C, 2, 2)
                            dve.tensor_tensor(ohw[:, :, :, :], oh2[:, :, :, :],
                                              w01[:, :, :].unsqueeze(3).broadcast_to([P, 2, G, E0]),
                                              ALU.mult).then_inc(sem("ohw"), 1)
                            after(dve, "ohw", C)
                            after(dve, "wo_ps", W.before(1))
                            dve.tensor_tensor(wo[:, :, WCOL:WCOL + E0], ohw[:, 0, :, :], ohw[:, 1, :, :],
                                              ALU.add).then_inc(sem("wcat"), 1)
                    if s == 7:
                        if B.live():
                            attended("B", B)
                            after(dve, "x1", B.before(1))
                            dve.tensor_scalar(zneg[:, :, :], z["B"][:, :, :], 0.0, None, ALU.min).then_inc(sem("zneg"), 1)
                        if at["e"].live():
                            scores("E", at["e"])

            body(dve, {1: mask_rows, 4: first_weights, 7: biases_and_weights})

        @block.tensor
        def _(pe):
            pe.wait_ge(sem("ident"), 1)
            pe.wait_ge(sem("graph_consts"), 1)

            def columns():
                pe.wait_ge(sem("mix_in"), 16 * NMIXIN)
                pe.transpose(YB[:, 0:E1], rw_row[:, :], ident[0:E1, 0:E1])
                pe.transpose(YB[:, E1:E1 + E0 * C0], b1row[:, :], ident[0:E0 * C0, 0:E0 * C0])
                pe.transpose(YB[:, E1 + E0 * C0:E1 + E0 * C0 + E0], b2row[:, :],
                             ident[0:E0, 0:E0]).then_inc(sem("cols_ps"), 1)

            def weights():
                columns()
                pe.wait_ge(sem("cols"), 1)
                pe.wait_ge(sem("w1_lo"), 1)
                pe.wait_ge(sem("w2_lo"), 1)

            def second_weights():
                pe.wait_ge(sem("biases"), 1)
                pe.wait_ge(sem("v_lo"), 1)

            def turn(bank, src, done, n=P):
                for q in range(G):
                    last = pe.transpose(bank[0:n, q * P:(q + 1) * P], src[:, q, :], ident[:, :])
                last.then_inc(sem(done), 1)

            def rows(k, g):
                after(pe, f"xn{k}", g)
                turn(TPB[k], xn[k], f"xn_ps{k}")

            def front_h(k, g):
                l = "AE".index(k)
                after(pe, f"xnT{k}", g)
                for q in range(G):
                    to = h3(k)[:, q, :] if q < G - 1 else h4(k)
                    last = pe.matmul(to, xnT[k][:, q * P:(q + 1) * P], Wg[l][:, :], start=(q in (0, G - 1)),
                                     stop=(q >= G - 2), skip_group_check=True)
                last.then_inc(sem(f"h_ps{k}"), 1)

            def front_s(k, g):
                l = "AE".index(k)
                pe.matmul(SB[:, :], wa2rep[l][:, :], xnT[k][:, :], start=True, stop=False)
                pe.matmul(g4(SB), identb[:, :], mask[l][:, :].unsqueeze(1).broadcast_to([P, G, P]), start=False,
                          stop=True).then_inc(sem(f"s_ps{k}"), 1)

            def attend(k, src, g):
                after(pe, f"prT{k}", g)
                for q in range(G):
                    last = pe.matmul(HB[:, q * P:(q + 1) * P], prT[k][:, q * P:(q + 1) * P], hg[src][g.par][:, q, 0:P],
                                     start=(q == 0), stop=(q == G - 1), skip_group_check=True)
                last.then_inc(sem(f"att_ps{k}"), 1)

            def route(k, g, w, n):
                after(pe, f"xnT{k}", g)
                for q in range(G):
                    last = pe.matmul(SB[:, q * n:(q + 1) * n], xnT[k][:, q * P:(q + 1) * P], w[:, :],
                                     start=(q == 0), stop=(q == G - 1), skip_group_check=True)
                last.then_inc(sem(f"lg_ps{k}"), 1)

            @each
            def body(j, p):
                at = stages(j, p)
                A, B, C, D, E, F, M, O, W = (at[k] for k in "ABCDEFMOW")

                def split(out_, w_hi, w_lo, k, g, stop, done):
                    hi, lo = xhi[k][g.par], xlo[k][g.par]
                    pe.matmul(out_[:, :], w_hi, hi[:, :], start=True, stop=False)
                    pe.matmul(out_[:, :], w_lo, hi[:, :], start=False, stop=False)
                    last = pe.matmul(out_[:, :], w_hi, lo[:, :], start=False, stop=stop)
                    if stop:
                        last.then_inc(sem(done), 1)

                def first_layer(s, c):
                    n = C0 * s + c
                    if c == 0:
                        after(pe, "gelu", D, E0 * C0, C0 * s)
                    else:
                        after(pe, "rlo", M, NCH, s)
                    w = slice(n * P, (n + 1) * P)
                    split(half_bank(s, c), w1hi[:, w], w1lo[:, w], "C", D, True, "d_l1")

                def second_layer(g, e):
                    if e == 0:
                        after(pe, "ym", g.before(1), E0, E0)
                    else:
                        after(pe, "ym", g, E0, e)
                    for c in range(C0):
                        after(pe, f"hhi{c}", g, E0, e + 1)
                        hi, n = hhi[e % 2][c], C0 * e + c
                        pe.matmul(YB[:, :], w2hi[:, n, :], hi[:, :], start=(c == 0), stop=False)
                        pe.matmul(YB[:, :], w2lo[:, n, :], hi[:, :], start=False, stop=False)
                    for c in range(C0):
                        after(pe, f"hlo{c}", g, E0, e + 1)
                        last = pe.matmul(YB[:, :], w2hi[:, C0 * e + c, :], hlo[e % 2][c][:, :], start=False,
                                         stop=(c == C0 - 1))
                    last.then_inc(sem("d_l2"), 1)

                users = {
                    "TP0": (("hA", at["a"]), ("hE", at["e"]), ("xnTA", A), ("fin", O), ("x2", E), ("xnTC", C), ("woT", W)),
                    "TP1": (("hE", at["e"]), ("prTF", F), ("prTB", B), ("xnTF", F), ("xnTE", E)),
                    "H": (("hA", at["a"]), ("zF", F), ("zB", B)),
                    "S": (("rawA", at["a"]), ("rawE", at["e"]), ("lgC", C), ("lgF", F)),
                }

                def free(bank, n):
                    for m, (name, g) in enumerate(users[bank]):
                        after(pe, name, g if m < n else g.before(1))

                def second_chunk(g, c):
                    if c == 0:
                        after(pe, "oT", g.before(1))
                    after(pe, "rlo", g, NCH, c + 1)
                    pe.matmul(OB[:, :], v2hi[:, c, :], rhi[c % 2][:, :], start=(c == 0), stop=False)
                    pe.matmul(OB[:, :], v2lo[:, c, :], rhi[c % 2][:, :], start=False, stop=False)
                    last = pe.matmul(OB[:, :], v2hi[:, c, :], rlo[c % 2][:, :], start=False, stop=False)
                    if c == NCH - 1:
                        last = pe.matmul(OB[:, :], c2[:, :], woT[g.par][0:2 * E1, :], start=False, stop=True)
                    last.then_inc(sem("m_l2"), 1)

                for s in range(SLOTS):
                    if D.live():
                        if s == 0:
                            after(pe, "xloC", D)
                        first_layer(s, 0)
                        first_layer(s, 1)
                    chunk = (M.before(1), NCH - 1) if s == 0 else (M, s - 1)
                    if chunk[0].live() and D.live():
                        second_chunk(*chunk)
                    if s == 1:
                        a, b = at["a"], at["e"]
                        if a.live():
                            free("H", 0)
                            free("TP0", 0)
                            front_h("A", a)
                        if b.live():
                            free("TP1", 0)
                            for m, (name, g) in enumerate(users["TP0"]):
                                if m != 0:
                                    after(pe, name, g.before(1))
                            front_h("E", b)
                        if a.live():
                            free("S", 0)
                            front_s("A", a)
                    if M.live():
                        if s == 0:
                            after(pe, "xloF", M)
                            after(pe, "woT", W.before(1))
                        if D.live():
                            after(pe, "gelu", D, E0 * C0, C0 * s + 1)
                        else:
                            after(pe, "gelu", D.before(1), E0 * C0, E0 * C0)
                        after(pe, "rlo", M, NCH, max(s - 1, 0))
                        w = slice(s * P, (s + 1) * P)
                        zb = chunk_bank(s)
                        split(zb, v1hi[:, w], v1lo[:, w], "F", M, False, None)
                        pe.matmul(zb[:, :], sel[:, w], woT[M.par][0:WCOL, :], start=False, stop=True).then_inc(sem("m_l1"), 1)
                    if chunk[0].live() and not D.live():
                        second_chunk(*chunk)
                    g, e = (D.before(1), SLOTS - 1) if s == 0 else (D, s - 1)
                    if g.live():
                        second_layer(g, e)
                    if s == 1 and at["e"].live():
                        free("S", 1)
                        front_s("E", at["e"])
                    if s == 1 and A.live():
                        free("TP0", 2)
                        rows("A", A)
                    if s == 2:
                        if F.live():
                            free("TP1", 1)
                            after(pe, "prF", F)
                            turn(TP1, pr["F"], "pr_psF")
                        if O.live():
                            after(pe, "oT", O)
                            free("TP0", 3)
                            for q in range(G):
                                last = pe.transpose(TP0[:, q * P:(q + 1) * P], oT[:, q * P:(q + 1) * P], ident[:, :])
                            last.then_inc(sem("out_ps"), 1)
                    if s == 3:
                        if F.live():
                            free("H", 1)
                            attend("F", "E", F)
                        if E.live():
                            free("TP0", 4)
                            after(pe, "ysum", E, SLOTS - 1, SLOTS - 1)
                            for q in range(G):
                                last = pe.transpose(TP0[:, q * P:(q + 1) * P], acc[E.par][:, q * P:(q + 1) * P], ident[:, :])
                            last.then_inc(sem("y_ps"), 1)
                    if s == 4:
                        if C.live():
                            free("TP0", 5)
                            rows("C", C)
                        if B.live():
                            free("TP1", 2)
                            after(pe, "prB", B)
                            turn(TP1, pr["B"], "pr_psB")
                    if s == 5:
                        if F.live():
                            free("TP1", 3)
                            rows("F", F)
                        if C.live():
                            free("S", 2)
                            route("C", C, wr_sb, E0)
                    if s == 6:
                        if F.live():
                            free("S", 3)
                            route("F", F, rwT, E1)
                        if B.live():
                            free("H", 2)
                            attend("B", "A", B)
                    if s == 7:
                        if E.live():
                            free("TP1", 4)
                            rows("E", E)
                        if W.live():
                            free("TP0", 6)
                            after(pe, "wcat", C)
                            after(pe, "ohc", F)
                            turn(TP0, wo, "wo_ps")

            body(pe, {4: weights, 8: second_weights})


_INS = ["x", "adj", "L0_gnn_W", "L0_gnn_a", "L0_ffn_gamma", "L0_ffn_beta", "L0_ffn_Wr", "L0_ffn_br", "L0_ffn_W1",
        "L0_ffn_b1", "L0_ffn_W2", "L0_ffn_b2", "L1_gnn_W", "L1_gnn_a", "L1_ffn_router_w", "L1_ffn_router_b",
        "L1_ffn_W1", "L1_ffn_b1", "L1_ffn_W2", "L1_ffn_b2"]


def kernel(**inputs):
    import numpy as np
    import concourse.bacc as bacc
    from concourse.bass_utils import run_bass_kernel_spmd

    nc = bacc.Bacc("TRN2", target_bir_lowering=False, num_devices=1)
    arrays, args = {}, []
    for name in _INS:
        a = np.ascontiguousarray(inputs[name])
        arrays[f"in_{name}"] = a
        args.append(nc.dram_tensor(f"in_{name}", a.shape, mybir.dt.from_np(a.dtype), kind="ExternalInput").ap())
    o = nc.dram_tensor("out", [NGRAPH, P, P], F32, kind="ExternalOutput").ap()
    program(nc, *args, o)
    r = run_bass_kernel_spmd(nc, [arrays], core_ids=[0])
    return r.results[0]["out"]
```
